# Optimizing a Trainium2 kernel written in Bass

```python
import numpy as np
import jax
import jax.numpy as jnp

def _softmax(x, axis=-1):
    return jax.nn.softmax(x, axis=axis)

def _gelu(x):
    return jax.nn.gelu(x, approximate=True)

def _silu(x):
    return jax.nn.silu(x)

def _sigmoid(x):
    return jax.nn.sigmoid(x)

def _layernorm(x, axis=-1, eps=1e-05):
    m = jnp.mean(x, axis=axis, keepdims=True)
    v = jnp.var(x, axis=axis, keepdims=True)
    return (x - m) / jnp.sqrt(v + eps)

def _scatter_add(tgt, idx, src, axis=0):
    return tgt.at[idx].add(src)

def _segment_sum(src, seg, n):
    return jax.ops.segment_sum(src, seg, n)
kernel_name = 'mk_dlrm_tower_d1_rec_r8_952143'

def setup_inputs(seed: int=0):
    np.random.seed(seed)
    _w = jnp.asarray

    def _rec_inputs():
        import jax
        import jax.numpy as jnp
        _tk = jax.random.key(seed)
        dense_ctx = jax.random.normal(jax.random.fold_in(_tk, 190), (1024, 16), jnp.float32)
        ids = jnp.stack([jax.random.randint(jax.random.fold_in(_tk, 200 + f), (1024,), 0, v, jnp.int32) for f, v in enumerate([1250, 1250, 1250, 1000, 1250, 1250, 1000, 12500, 1000, 12500, 1250, 1000, 1250, 1000, 1250, 1250, 1250, 1000, 12500, 12500, 1250, 12500, 1250, 1250, 1250, 12500, 1250, 1000, 1250, 1250, 1000, 1250, 1000, 1000, 1000, 1000, 1250, 1250, 1250, 1000, 1000, 1000, 1000, 1000, 1000, 1000, 1000, 1000, 1000, 1000])], axis=1)
        tbl_0 = 0.05 * jax.random.normal(jax.random.fold_in(_tk, 500 + 0), (1250, 300), jnp.float32)
        tbl_1 = 0.05 * jax.random.normal(jax.random.fold_in(_tk, 500 + 1), (1250, 300), jnp.float32)
        tbl_2 = 0.05 * jax.random.normal(jax.random.fold_in(_tk, 500 + 2), (1250, 300), jnp.float32)
        tbl_3 = 0.05 * jax.random.normal(jax.random.fold_in(_tk, 500 + 3), (1000, 300), jnp.float32)
        tbl_4 = 0.05 * jax.random.normal(jax.random.fold_in(_tk, 500 + 4), (1250, 300), jnp.float32)
        tbl_5 = 0.05 * jax.random.normal(jax.random.fold_in(_tk, 500 + 5), (1250, 300), jnp.float32)
        tbl_6 = 0.05 * jax.random.normal(jax.random.fold_in(_tk, 500 + 6), (1000, 300), jnp.float32)
        tbl_7 = 0.05 * jax.random.normal(jax.random.fold_in(_tk, 500 + 7), (12500, 300), jnp.float32)
        tbl_8 = 0.05 * jax.random.normal(jax.random.fold_in(_tk, 500 + 8), (1000, 300), jnp.float32)
        tbl_9 = 0.05 * jax.random.normal(jax.random.fold_in(_tk, 500 + 9), (12500, 300), jnp.float32)
        tbl_10 = 0.05 * jax.random.normal(jax.random.fold_in(_tk, 500 + 10), (1250, 300), jnp.float32)
        tbl_11 = 0.05 * jax.random.normal(jax.random.fold_in(_tk, 500 + 11), (1000, 300), jnp.float32)
        tbl_12 = 0.05 * jax.random.normal(jax.random.fold_in(_tk, 500 + 12), (1250, 300), jnp.float32)
        tbl_13 = 0.05 * jax.random.normal(jax.random.fold_in(_tk, 500 + 13), (1000, 300), jnp.float32)
        tbl_14 = 0.05 * jax.random.normal(jax.random.fold_in(_tk, 500 + 14), (1250, 300), jnp.float32)
        tbl_15 = 0.05 * jax.random.normal(jax.random.fold_in(_tk, 500 + 15), (1250, 300), jnp.float32)
        tbl_16 = 0.05 * jax.random.normal(jax.random.fold_in(_tk, 500 + 16), (1250, 300), jnp.float32)
        tbl_17 = 0.05 * jax.random.normal(jax.random.fold_in(_tk, 500 + 17), (1000, 300), jnp.float32)
        tbl_18 = 0.05 * jax.random.normal(jax.random.fold_in(_tk, 500 + 18), (12500, 300), jnp.float32)
        tbl_19 = 0.05 * jax.random.normal(jax.random.fold_in(_tk, 500 + 19), (12500, 300), jnp.float32)
        tbl_20 = 0.05 * jax.random.normal(jax.random.fold_in(_tk, 500 + 20), (1250, 300), jnp.float32)
        tbl_21 = 0.05 * jax.random.normal(jax.random.fold_in(_tk, 500 + 21), (12500, 300), jnp.float32)
        tbl_22 = 0.05 * jax.random.normal(jax.random.fold_in(_tk, 500 + 22), (1250, 300), jnp.float32)
        tbl_23 = 0.05 * jax.random.normal(jax.random.fold_in(_tk, 500 + 23), (1250, 300), jnp.float32)
        tbl_24 = 0.05 * jax.random.normal(jax.random.fold_in(_tk, 500 + 24), (1250, 300), jnp.float32)
        tbl_25 = 0.05 * jax.random.normal(jax.random.fold_in(_tk, 500 + 25), (12500, 300), jnp.float32)
        tbl_26 = 0.05 * jax.random.normal(jax.random.fold_in(_tk, 500 + 26), (1250, 300), jnp.float32)
        tbl_27 = 0.05 * jax.random.normal(jax.random.fold_in(_tk, 500 + 27), (1000, 300), jnp.float32)
        tbl_28 = 0.05 * jax.random.normal(jax.random.fold_in(_tk, 500 + 28), (1250, 300), jnp.float32)
        tbl_29 = 0.05 * jax.random.normal(jax.random.fold_in(_tk, 500 + 29), (1250, 300), jnp.float32)
        tbl_30 = 0.05 * jax.random.normal(jax.random.fold_in(_tk, 500 + 30), (1000, 300), jnp.float32)
        tbl_31 = 0.05 * jax.random.normal(jax.random.fold_in(_tk, 500 + 31), (1250, 300), jnp.float32)
        tbl_32 = 0.05 * jax.random.normal(jax.random.fold_in(_tk, 500 + 32), (1000, 300), jnp.float32)
        tbl_33 = 0.05 * jax.random.normal(jax.random.fold_in(_tk, 500 + 33), (1000, 300), jnp.float32)
        tbl_34 = 0.05 * jax.random.normal(jax.random.fold_in(_tk, 500 + 34), (1000, 300), jnp.float32)
        tbl_35 = 0.05 * jax.random.normal(jax.random.fold_in(_tk, 500 + 35), (1000, 300), jnp.float32)
        tbl_36 = 0.05 * jax.random.normal(jax.random.fold_in(_tk, 500 + 36), (1250, 300), jnp.float32)
        tbl_37 = 0.05 * jax.random.normal(jax.random.fold_in(_tk, 500 + 37), (1250, 300), jnp.float32)
        tbl_38 = 0.05 * jax.random.normal(jax.random.fold_in(_tk, 500 + 38), (1250, 300), jnp.float32)
        tbl_39 = 0.05 * jax.random.normal(jax.random.fold_in(_tk, 500 + 39), (1000, 300), jnp.float32)
        tbl_40 = 0.05 * jax.random.normal(jax.random.fold_in(_tk, 500 + 40), (1000, 300), jnp.float32)
        tbl_41 = 0.05 * jax.random.normal(jax.random.fold_in(_tk, 500 + 41), (1000, 300), jnp.float32)
        tbl_42 = 0.05 * jax.random.normal(jax.random.fold_in(_tk, 500 + 42), (1000, 300), jnp.float32)
        tbl_43 = 0.05 * jax.random.normal(jax.random.fold_in(_tk, 500 + 43), (1000, 300), jnp.float32)
        tbl_44 = 0.05 * jax.random.normal(jax.random.fold_in(_tk, 500 + 44), (1000, 300), jnp.float32)
        tbl_45 = 0.05 * jax.random.normal(jax.random.fold_in(_tk, 500 + 45), (1000, 300), jnp.float32)
        tbl_46 = 0.05 * jax.random.normal(jax.random.fold_in(_tk, 500 + 46), (1000, 300), jnp.float32)
        tbl_47 = 0.05 * jax.random.normal(jax.random.fold_in(_tk, 500 + 47), (1000, 300), jnp.float32)
        tbl_48 = 0.05 * jax.random.normal(jax.random.fold_in(_tk, 500 + 48), (1000, 300), jnp.float32)
        tbl_49 = 0.05 * jax.random.normal(jax.random.fold_in(_tk, 500 + 49), (1000, 300), jnp.float32)
        _rk = jax.random.fold_in(_tk, 7)
        r_label_embedding = -1.64977e-06 + 0.999867 * jax.random.normal(jax.random.fold_in(_rk, 101), (1024, 200, 300), jnp.float32)
        W_top1 = 0.0680414 * jax.random.normal(jax.random.fold_in(_tk, 801), (216, 512), jnp.float32)
        W_top2 = 0.0441942 * jax.random.normal(jax.random.fold_in(_tk, 802), (512, 256), jnp.float32)
        W_top3 = 0.0625 * jax.random.normal(jax.random.fold_in(_tk, 803), (256, 1), jnp.float32)
        b_top1 = jnp.zeros((512,), jnp.float32)
        b_top2 = jnp.zeros((256,), jnp.float32)
        return (dense_ctx, ids, tbl_0, tbl_1, tbl_2, tbl_3, tbl_4, tbl_5, tbl_6, tbl_7, tbl_8, tbl_9, tbl_10, tbl_11, tbl_12, tbl_13, tbl_14, tbl_15, tbl_16, tbl_17, tbl_18, tbl_19, tbl_20, tbl_21, tbl_22, tbl_23, tbl_24, tbl_25, tbl_26, tbl_27, tbl_28, tbl_29, tbl_30, tbl_31, tbl_32, tbl_33, tbl_34, tbl_35, tbl_36, tbl_37, tbl_38, tbl_39, tbl_40, tbl_41, tbl_42, tbl_43, tbl_44, tbl_45, tbl_46, tbl_47, tbl_48, tbl_49, r_label_embedding, W_top1, b_top1, W_top2, b_top2, W_top3)
    dense_ctx, ids, tbl_0, tbl_1, tbl_2, tbl_3, tbl_4, tbl_5, tbl_6, tbl_7, tbl_8, tbl_9, tbl_10, tbl_11, tbl_12, tbl_13, tbl_14, tbl_15, tbl_16, tbl_17, tbl_18, tbl_19, tbl_20, tbl_21, tbl_22, tbl_23, tbl_24, tbl_25, tbl_26, tbl_27, tbl_28, tbl_29, tbl_30, tbl_31, tbl_32, tbl_33, tbl_34, tbl_35, tbl_36, tbl_37, tbl_38, tbl_39, tbl_40, tbl_41, tbl_42, tbl_43, tbl_44, tbl_45, tbl_46, tbl_47, tbl_48, tbl_49, r_label_embedding, W_top1, b_top1, W_top2, b_top2, W_top3 = _rec_inputs()

    def _L0_rec_setup():
        import jax, jax.numpy as jnp
        import numpy as np
        E, U, C, T, N, B, K = (300, 300, 4, 8, 50, 512, 200)
        P = E * (E - 1) // 2
        PAD = jnp.float32(-2 ** 32 + 1)

        def _attn_pool(x, mask, w_a, b_a, w_b):
            score = jnp.exp((x @ w_a + b_a) @ w_b)
            score = jnp.where(mask == 0, PAD, score)
            p = jax.nn.softmax(score, axis=1)
            return jnp.einsum('bne,bn->be', x, p[..., 0])
        key = jax.random.key(seed)
        ks = jax.random.split(key, 20)
        s = 0.02
        return {'x': jax.random.normal(ks[0], (B, N, E), jnp.float32), 'label_embedding': jax.random.normal(ks[1], (B, K, U), jnp.float32), 'w1': jax.random.normal(ks[2], (E, T), jnp.float32) * s, 'b1': jnp.zeros((T,), jnp.float32), 'w2': jax.random.normal(ks[3], (T, 1), jnp.float32) * s, 'w3': jax.random.normal(ks[4], (E, T), jnp.float32) * s, 'b3': jnp.zeros((T,), jnp.float32), 'w4': jax.random.normal(ks[5], (T, 1), jnp.float32) * s, 'w5': jax.random.normal(ks[6], (2 * E, E), jnp.float32) * s, 'b5': jnp.zeros((E,), jnp.float32), 'w6': jax.random.normal(ks[7], (E, E), jnp.float32) * s, 'b6': jnp.zeros((E,), jnp.float32), 'w7': jax.random.normal(ks[8], (P, E), jnp.float32) * s, 'b7': jnp.zeros((E,), jnp.float32), 'w8': jax.random.normal(ks[9], (2 * E, U), jnp.float32) * s, 'b8': jnp.zeros((U,), jnp.float32), 'v': jax.random.uniform(ks[10], (E, C), jnp.float32)}
    _L0_rec_all = _L0_rec_setup()
    _L0_rec_in = {k: v for k, v in _L0_rec_all.items() if k in ('w1', 'b1', 'w2', 'w3', 'b3', 'w4', 'w5', 'b5', 'w6', 'b6', 'w7', 'b7', 'w8', 'b8', 'v')}
    del _L0_rec_all
    return {'dense_ctx': dense_ctx, 'ids': ids, 'tbl_0': tbl_0, 'tbl_1': tbl_1, 'tbl_2': tbl_2, 'tbl_3': tbl_3, 'tbl_4': tbl_4, 'tbl_5': tbl_5, 'tbl_6': tbl_6, 'tbl_7': tbl_7, 'tbl_8': tbl_8, 'tbl_9': tbl_9, 'tbl_10': tbl_10, 'tbl_11': tbl_11, 'tbl_12': tbl_12, 'tbl_13': tbl_13, 'tbl_14': tbl_14, 'tbl_15': tbl_15, 'tbl_16': tbl_16, 'tbl_17': tbl_17, 'tbl_18': tbl_18, 'tbl_19': tbl_19, 'tbl_20': tbl_20, 'tbl_21': tbl_21, 'tbl_22': tbl_22, 'tbl_23': tbl_23, 'tbl_24': tbl_24, 'tbl_25': tbl_25, 'tbl_26': tbl_26, 'tbl_27': tbl_27, 'tbl_28': tbl_28, 'tbl_29': tbl_29, 'tbl_30': tbl_30, 'tbl_31': tbl_31, 'tbl_32': tbl_32, 'tbl_33': tbl_33, 'tbl_34': tbl_34, 'tbl_35': tbl_35, 'tbl_36': tbl_36, 'tbl_37': tbl_37, 'tbl_38': tbl_38, 'tbl_39': tbl_39, 'tbl_40': tbl_40, 'tbl_41': tbl_41, 'tbl_42': tbl_42, 'tbl_43': tbl_43, 'tbl_44': tbl_44, 'tbl_45': tbl_45, 'tbl_46': tbl_46, 'tbl_47': tbl_47, 'tbl_48': tbl_48, 'tbl_49': tbl_49, 'r_label_embedding': r_label_embedding, 'W_top1': W_top1, 'b_top1': b_top1, 'W_top2': W_top2, 'b_top2': b_top2, 'W_top3': W_top3, 'L0_rec_w1': _L0_rec_in['w1'], 'L0_rec_b1': _L0_rec_in['b1'], 'L0_rec_w2': _L0_rec_in['w2'], 'L0_rec_w3': _L0_rec_in['w3'], 'L0_rec_b3': _L0_rec_in['b3'], 'L0_rec_w4': _L0_rec_in['w4'], 'L0_rec_w5': _L0_rec_in['w5'], 'L0_rec_b5': _L0_rec_in['b5'], 'L0_rec_w6': _L0_rec_in['w6'], 'L0_rec_b6': _L0_rec_in['b6'], 'L0_rec_w7': _L0_rec_in['w7'], 'L0_rec_b7': _L0_rec_in['b7'], 'L0_rec_w8': _L0_rec_in['w8'], 'L0_rec_b8': _L0_rec_in['b8'], 'L0_rec_v': _L0_rec_in['v']}

def reference(dense_ctx, ids, tbl_0, tbl_1, tbl_2, tbl_3, tbl_4, tbl_5, tbl_6, tbl_7, tbl_8, tbl_9, tbl_10, tbl_11, tbl_12, tbl_13, tbl_14, tbl_15, tbl_16, tbl_17, tbl_18, tbl_19, tbl_20, tbl_21, tbl_22, tbl_23, tbl_24, tbl_25, tbl_26, tbl_27, tbl_28, tbl_29, tbl_30, tbl_31, tbl_32, tbl_33, tbl_34, tbl_35, tbl_36, tbl_37, tbl_38, tbl_39, tbl_40, tbl_41, tbl_42, tbl_43, tbl_44, tbl_45, tbl_46, tbl_47, tbl_48, tbl_49, r_label_embedding, W_top1, b_top1, W_top2, b_top2, W_top3, L0_rec_w1, L0_rec_b1, L0_rec_w2, L0_rec_w3, L0_rec_b3, L0_rec_w4, L0_rec_w5, L0_rec_b5, L0_rec_w6, L0_rec_b6, L0_rec_w7, L0_rec_b7, L0_rec_w8, L0_rec_b8, L0_rec_v):
    import jax
    import jax.numpy as jnp

    def _L0_rec_ref(x, label_embedding, w1, b1, w2, w3, b3, w4, w5, b5, w6, b6, w7, b7, w8, b8, v):
        import jax, jax.numpy as jnp
        import numpy as np
        E, U, C, T, N, B, K = (300, 300, 4, 8, 50, 512, 200)
        P = E * (E - 1) // 2
        PAD = jnp.float32(-2 ** 32 + 1)

        def _attn_pool(x, mask, w_a, b_a, w_b):
            score = jnp.exp((x @ w_a + b_a) @ w_b)
            score = jnp.where(mask == 0, PAD, score)
            p = jax.nn.softmax(score, axis=1)
            return jnp.einsum('bne,bn->be', x, p[..., 0])
        mask = jnp.sign(jnp.sum(jnp.abs(x), axis=2))[..., None]
        q1 = _attn_pool(x, mask, w1, b1, w2)
        q2 = _attn_pool(x, mask, w3, b3, w4)
        h = jnp.concatenate([q1, q2], axis=1) @ w5 + b5
        f6 = h @ w6 + b6
        iu, ju = jnp.triu_indices(E, k=1)
        g = (v @ v.T)[iu, ju]
        cross = h[:, iu] * h[:, ju] * g
        f7 = cross @ w7 + b7
        out8 = jnp.concatenate([f6, f7], axis=1) @ w8 + b8
        return jnp.einsum('bu,bku->bk', out8, label_embedding)
    e = jnp.stack([tbl_0[ids[:, 0]], tbl_1[ids[:, 1]], tbl_2[ids[:, 2]], tbl_3[ids[:, 3]], tbl_4[ids[:, 4]], tbl_5[ids[:, 5]], tbl_6[ids[:, 6]], tbl_7[ids[:, 7]], tbl_8[ids[:, 8]], tbl_9[ids[:, 9]], tbl_10[ids[:, 10]], tbl_11[ids[:, 11]], tbl_12[ids[:, 12]], tbl_13[ids[:, 13]], tbl_14[ids[:, 14]], tbl_15[ids[:, 15]], tbl_16[ids[:, 16]], tbl_17[ids[:, 17]], tbl_18[ids[:, 18]], tbl_19[ids[:, 19]], tbl_20[ids[:, 20]], tbl_21[ids[:, 21]], tbl_22[ids[:, 22]], tbl_23[ids[:, 23]], tbl_24[ids[:, 24]], tbl_25[ids[:, 25]], tbl_26[ids[:, 26]], tbl_27[ids[:, 27]], tbl_28[ids[:, 28]], tbl_29[ids[:, 29]], tbl_30[ids[:, 30]], tbl_31[ids[:, 31]], tbl_32[ids[:, 32]], tbl_33[ids[:, 33]], tbl_34[ids[:, 34]], tbl_35[ids[:, 35]], tbl_36[ids[:, 36]], tbl_37[ids[:, 37]], tbl_38[ids[:, 38]], tbl_39[ids[:, 39]], tbl_40[ids[:, 40]], tbl_41[ids[:, 41]], tbl_42[ids[:, 42]], tbl_43[ids[:, 43]], tbl_44[ids[:, 44]], tbl_45[ids[:, 45]], tbl_46[ids[:, 46]], tbl_47[ids[:, 47]], tbl_48[ids[:, 48]], tbl_49[ids[:, 49]]], axis=1)
    z = _L0_rec_ref(e, r_label_embedding, L0_rec_w1, L0_rec_b1, L0_rec_w2, L0_rec_w3, L0_rec_b3, L0_rec_w4, L0_rec_w5, L0_rec_b5, L0_rec_w6, L0_rec_b6, L0_rec_w7, L0_rec_b7, L0_rec_w8, L0_rec_b8, L0_rec_v)
    z = z.reshape(z.shape[0], -1)
    h = jnp.concatenate([z, dense_ctx], axis=1)
    h = jnp.maximum(h @ W_top1 + b_top1, 0.0)
    h = jnp.maximum(h @ W_top2 + b_top2, 0.0)
    y = h @ W_top3
    return y

_drawn_inputs = setup_inputs


def setup_inputs(seed=0):
    import zlib

    import numpy as np

    out = dict(_drawn_inputs(seed))
    spreads = {'b_top1': (0.0, 0.473),
     'b_top2': (0.0, 0.1),
     'L0_rec_b1': (0.0, 0.8),
     'L0_rec_b3': (0.0, 0.8),
     'L0_rec_b5': (0.0, 0.1),
     'L0_rec_b6': (0.0, 0.1),
     'L0_rec_b7': (0.0, 0.1),
     'L0_rec_b8': (0.0, 0.1)}
    factors = {'tbl_0': 8.0,
     'tbl_1': 8.0,
     'tbl_2': 8.0,
     'tbl_3': 8.0,
     'tbl_4': 8.0,
     'tbl_5': 8.0,
     'tbl_6': 8.0,
     'tbl_7': 8.0,
     'tbl_8': 8.0,
     'tbl_9': 8.0,
     'tbl_10': 8.0,
     'tbl_11': 8.0,
     'tbl_12': 8.0,
     'tbl_13': 8.0,
     'tbl_14': 8.0,
     'tbl_15': 8.0,
     'tbl_16': 8.0,
     'tbl_17': 8.0,
     'tbl_18': 8.0,
     'tbl_19': 8.0,
     'tbl_20': 8.0,
     'tbl_21': 8.0,
     'tbl_22': 8.0,
     'tbl_23': 8.0,
     'tbl_24': 8.0,
     'tbl_25': 8.0,
     'tbl_26': 8.0,
     'tbl_27': 8.0,
     'tbl_28': 8.0,
     'tbl_29': 8.0,
     'tbl_30': 8.0,
     'tbl_31': 8.0,
     'tbl_32': 8.0,
     'tbl_33': 8.0,
     'tbl_34': 8.0,
     'tbl_35': 8.0,
     'tbl_36': 8.0,
     'tbl_37': 8.0,
     'tbl_38': 8.0,
     'tbl_39': 8.0,
     'tbl_40': 8.0,
     'tbl_41': 8.0,
     'tbl_42': 8.0,
     'tbl_43': 8.0,
     'tbl_44': 8.0,
     'tbl_45': 8.0,
     'tbl_46': 8.0,
     'tbl_47': 8.0,
     'tbl_48': 8.0,
     'tbl_49': 8.0,
     'L0_rec_w1': 8.0,
     'L0_rec_w2': 8.0,
     'L0_rec_w3': 8.0,
     'L0_rec_w4': 8.0,
     'L0_rec_w5': 5.189}
    for name, (base, spread) in spreads.items():
        noise = np.random.default_rng([zlib.crc32(name.encode()), seed]).standard_normal(out[name].shape)
        drawn = base * np.exp(spread * noise) if base else spread * noise
        out[name] = jnp.asarray(drawn.astype(out[name].dtype))
    for name, factor in factors.items():
        out[name] = (out[name] * factor).astype(out[name].dtype)
    return out
```

```python
import concourse.bass as bass
import numpy as np
from concourse import mybir

BATCH, FEATS, EMB, KEYS = 1024, 50, 300, 200
DENSE, HID1, HID2, RANK, ATT = 16, 512, 256, 4, 8
VOCAB = [1250, 1250, 1250, 1000, 1250, 1250, 1000, 12500, 1000, 12500, 1250, 1000, 1250, 1000, 1250,
         1250, 1250, 1000, 12500, 12500, 1250, 12500, 1250, 1250, 1250, 12500, 1250, 1000, 1250, 1250,
         1000, 1250, 1000, 1000, 1000, 1000, 1250, 1250, 1250, 1000] + [1000] * 10
ROWS = sum(VOCAB)
PAD = float(np.float32(-2 ** 32 + 1))

P = 128
BT = BATCH // P
CH = EMB // 3
HALF = P // 2
XT = FEATS // 2
XB = 5
NXB = XT // XB
XW = EMB + 1

NEAR = P
FAR_D, FAR_I = EMB // 2 - 1 - NEAR, 6
FAR_T = EMB // FAR_I
OPP = EMB // 4
KT = EMB + FAR_T + 2
GK = 4
GROUPS = KT // GK
UN = 4
ITS = GROUPS // UN
KI = UN * GK
MAIN_ITS = EMB // KI
H2W = EMB + EMB // 2

SEGS = [3, 3, 2]
NBM = max(SEGS)
ZK = 10
ZITS = KEYS // (ZK * UN)

ACC, POOLED, TBANK, MISC = 0, 3, 4, 6


def pair_indices():
    i = np.zeros((KT, P), np.int64)
    j = np.zeros((KT, P), np.int64)
    ok = np.zeros((KT, P), bool)
    for t in range(EMB):
        i[t], j[t], ok[t] = t, (t + 1 + np.arange(P)) % EMB, True
    for m in range(FAR_T):
        for a in range(FAR_I):
            s = slice(FAR_D * a, FAR_D * (a + 1))
            i[EMB + m, s] = FAR_I * m + a
            j[EMB + m, s] = (FAR_I * m + a + NEAR + 1 + np.arange(FAR_D)) % EMB
            ok[EMB + m, s] = True
    for q in range(2):
        i[EMB + FAR_T + q, :OPP] = OPP * q + np.arange(OPP)
        j[EMB + FAR_T + q, :OPP] = OPP * q + np.arange(OPP) + EMB // 2
        ok[EMB + FAR_T + q, :OPP] = True
    return i, j, ok


def build(nc, t_table, t_ids, t_offs, t_le, t_w7, t_vi, t_vj, t_att, t_w5, t_w6, t_w8, t_bias,
          t_wt1, t_bt1, t_wt2, t_bt2, t_wt3, t_dense, t_ident, t_sel, out):
    f32, i32, u32 = mybir.dt.float32, mybir.dt.int32, mybir.dt.uint32
    ALU, ACT, AX = mybir.AluOpType, mybir.ActivationFunctionType, mybir.AxisListType

    from contextlib import ExitStack
    ctx = ExitStack()
    with ctx:
        def sb(name, shape, dt=f32):
            return ctx.enter_context(nc.sbuf_tensor(name, shape, dt))

        def sem(name):
            return ctx.enter_context(nc.semaphore(name))

        ids = sb("ids", [P, BT * 2 * XT], i32)
        offs = sb("offs", [P, XT], i32)
        idx = sb("idx", [P, 2, XT], i32)
        big = sb("big", [P, 2 * XT * XW])
        x = big[:, :].rearrange("p (s t w) -> p s t w", s=2, t=XT)
        le = big[:, 0:UN * ZK * EMB].rearrange("p (s k u) -> p s k u", s=UN, k=ZK)
        zc = big[:, UN * ZK * EMB:UN * ZK * EMB + BT * (KEYS + DENSE)].rearrange("p (t k) -> p t k", t=BT)
        pm = sb("pm", [P, XT * 2 * HALF])
        vi = pm[:, 0:KT * RANK]
        vj = pm[:, KT * RANK:2 * KT * RANK]
        gate = sb("gate", [P, KT])
        ident = sb("ident", [P, P])
        sel = sb("sel", [P, HALF])
        ones = sb("ones", [1, P])
        wv = sb("wv", [P, 2, XW])
        score = sb("score", [P, 2, XT])
        absum = sb("absum", [P, XT])
        iszero = sb("iszero", [P, XT], i32)
        padrow = sb("padrow", [P, XT])
        es = sb("es", [P, 2, XT])
        ew = sb("ew", [P, 2, XT])
        mx = sb("mx", [P, 2])
        mxo = sb("mxo", [P, 2])
        negmax = sb("negmax", [P, 2])
        rsum = sb("rsum", [P, 2])
        junkv = sb("junkv", [P, 4, EMB])
        junka = sb("junka", [P, EMB])
        q = sb("q", [P, 2 * BT, EMB])
        qT = sb("qT", [CH, 2, 3, 2, P])
        h2 = sb("h2", [P, BT, H2W])
        hT = sb("hT", [CH, 2, 3, P])
        f6 = sb("f6", [P, 2, EMB])
        f6T = sb("f6T", [CH, BT, 3, P])
        out8 = q[:, :, :].rearrange("p (t a) e -> p a t e", a=2)[:, 0, :, :]
        f7 = q[:, :, :].rearrange("p (t a) e -> p a t e", a=2)[:, 1, 0:NBM, :]
        f7T = sb("f7T", [CH, 2, 3, P])
        w5 = sb("w5", [CH, 6, EMB])
        w6 = sb("w6", [CH, 3, EMB])
        w8 = sb("w8", [CH, 6, EMB])
        bias = sb("bias", [1, 4, EMB])
        cross = sb("cross", [P, 4, NBM, P])
        w2rep = cross[0:ATT, 0:2, 0, :]
        w1row = cross[0:ATT, 2:4, :, :].rearrange("p a t b -> p a (t b)")[:, :, 0:XW]
        crossT = sb("crossT", [P, 4, NBM, P])
        w7 = sb("w7", [P, UN, GK, EMB])
        wt1 = sb("wt1", [108, 2, HID1])
        bt1 = sb("bt1", [P, HID1 // P])
        wt2 = sb("wt2", [P, HID1 // P, HID2])
        bt2 = sb("bt2", [P, HID2 // P])
        wt3 = sb("wt3", [P, HID2 // P])
        y1 = pm[:, 0:HID1].rearrange("p (c b) -> p c b", b=P)
        y2 = pm[:, HID1:HID1 + HID2].rearrange("p (c b) -> p c b", b=P)
        zT = pm[0:108, HID1 + HID2:HID1 + HID2 + 2 * P].rearrange("p (c b) -> p c b", b=P)
        yrow = pm[0:1, 2 * BATCH:3 * BATCH]
        ps = ctx.enter_context(nc.psum_tensor("ps", [P, 8, 512], f32))

        att_in = sem("att_in")
        v_in = sem("v_in")
        const_in = sem("const_in")
        x_in = [[sem(f"x_in{s}_{b}") for b in range(NXB)] for s in range(2)]
        w7_in = [sem(f"w7_in{g}") for g in range(UN)]
        le_in = [sem(f"le_in{g}") for g in range(UN)]
        dense_in = sem("dense_in")
        y_out = sem("y_out")
        idx_ready = sem("idx_ready")
        init_done = sem("init_done")
        wv_mm = sem("wv_mm")
        wv_ready = sem("wv_ready")
        g_step = sem("g_step")
        score_step = sem("score_step")
        abs_done = sem("abs_done")
        es_done = sem("es_done")
        att_step = sem("att_step")
        ew_done = sem("ew_done")
        pm_done = sem("pm_done")
        pooled = sem("pooled")
        rsum_done = sem("rsum_done")
        q_done = sem("q_done")
        prod = sem("prod")
        trans = sem("trans")
        scaled = sem("scaled")
        summed = sem("summed")
        zdone = sem("zdone")
        unit_mm = sem("unit_mm")
        unit_ev = sem("unit_ev")

        ATT_STEPS = 6
        SCORE_STEPS = (XT + 1) // 2
        seg_start = [sum(SEGS[:s]) for s in range(len(SEGS))]
        seg_tiles = [list(range(a, a + n)) for a, n in zip(seg_start, SEGS)]
        FIRST_HALVES = 2 * SEGS[0]
        PRE = 3 + 4

        block = ctx.enter_context(nc.Block())

        def pairs(tiles):
            return [tiles[a:a + 2] for a in range(0, len(tiles), 2)]

        def counter():
            state = [0]

            def unit():
                state[0] += 1
                return state[0] - 1
            return unit

        def walk(eng, s, step, after):
            if s == 0:
                for it in (0, 1):
                    step(it, None, (it, FIRST_HALVES % 2, FIRST_HALVES // 2, "first"))
                with eng.Fori(0, 4) as r:
                    for a in range(2):
                        n = FIRST_HALVES + 1 + a
                        for b in range(2):
                            step(r * 4 + (2 + 2 * a + b), None, (b, n % 2, r + n // 2, "steady"))
                for it in (18, 19):
                    step(it, None, (it - 18, 1, BT - 1, "steady"))
                for it in (20, 21):
                    step(it, None, (it - 20, 0, BT, "drain"))
                return
            prev = seg_tiles[s - 1]
            for j, tile in enumerate(prev):
                lo = ZITS * j
                if s == 1 and j == 0:
                    step(0, (tile, 0), None)
                    lo = 1
                with eng.Fori(lo, ZITS * (j + 1)) as it:
                    step(it, (tile, it - ZITS * j), None)
                if j:
                    after(prev[j - 1])
            with eng.Fori(ZITS * len(prev), MAIN_ITS) as it:
                step(it, None, None)
            after(prev[-1])
            for it in range(MAIN_ITS, ITS):
                step(it, None, None)

        def zbase(s):
            return sum(SEGS[:s - 1]) * ZITS

        @block.sync
        def _(sp):
            for dst, src in ((ids[:, :], t_ids), (offs[:, :], t_offs), (w2rep, t_att[:, :, 0:P]),
                             (w1row, t_att[:, :, P:P + XW]), (sel[:, :], t_sel),
                             (ident[:, :], t_ident), (bias[:, :, :], t_bias)):
                sp.dma_start(dst, src).then_inc(att_in, 16)
            sp.dma_start(vi, t_vi).then_inc(v_in, 16)
            sp.dma_start(vj, t_vj).then_inc(v_in, 16)
            for dst, src in ((w5[:, :, :], t_w5), (w6[:, :, :], t_w6), (w8[:, :, :], t_w8),
                             (wt1[:, :, :], t_wt1), (bt1[:, :], t_bt1), (wt2[:, :, :], t_wt2),
                             (bt2[:, :], t_bt2), (wt3[:, :], t_wt3)):
                sp.dma_start(dst, src).then_inc(const_in, 16)

            def load_le(tile, zstep, zglobal, g):
                if not isinstance(zglobal, int) or zglobal > 0:
                    sp.wait_ge(zdone, zglobal * UN + (g + 1 - UN))
                elif g == 0:
                    sp.wait_ge(pooled, 2 * BT * NXB)
                    sp.dma_start(zc[:, :, KEYS:], t_dense.rearrange("(t p) c -> p t c", p=P)).then_inc(dense_in, 16)
                rows = t_le[tile * P:(tile + 1) * P, bass.ds((zstep * UN + g) * (ZK * EMB), ZK * EMB)]
                sp.dma_start(le[:, g, :, :].rearrange("p k u -> p (k u)"), rows).then_inc(le_in[g], 16)

            for s, nb in enumerate(SEGS):
                def step(it, z, period, s=s):
                    for g in range(UN):
                        if s > 0 or not isinstance(it, int) or it > 0:
                            sp.wait_ge(summed, (it + s * ITS) * KI + (GK * (g + 1) - KI))
                        sp.dma_start(w7[:, g, :, :].rearrange("p k u -> p (k u)"),
                                     t_w7[bass.ds(it * UN + g, 1), :, :].rearrange("a p n -> (a p) n")
                                     ).then_inc(w7_in[g], 16)
                        if z:
                            tile, zstep = z
                            load_le(tile, zstep, zstep + (tile * ZITS), g)
                walk(sp, s, step, lambda tile: None)
            for tile in seg_tiles[-1]:
                with sp.Fori(0, ZITS) as zstep:
                    for g in range(UN):
                        load_le(tile, zstep, zstep + tile * ZITS, g)
            sp.wait_ge(unit_ev, total_units)
            sp.dma_start(out, yrow).then_inc(y_out, 16)
            sp.wait_ge(y_out, 16)

        @block.gpsimd
        def _(pool):
            nc.gpsimd.memset(ones[:, :], 1.0).then_inc(init_done, 1)
            nc.gpsimd.memset(padrow[:, :], PAD).then_inc(init_done, 1)
            nc.gpsimd.memset(x[:, :, :, EMB:XW], 1.0).then_inc(init_done, 1)
            pool.wait_ge(att_in, 7 * 16)

            def gather(slot, m, first):
                n = m * 2 + slot
                if not first:
                    pool.wait_ge(pooled, n * NXB - (2 * NXB - 1))
                nc.gpsimd.tensor_tensor(idx[:, slot, :], ids[:, bass.ds(n * XT, XT)], offs[:, :],
                                        ALU.add).then_inc(idx_ready, 1)
                pool.wait_ge(idx_ready, n + 1)
                for b in range(NXB):
                    if not first and b:
                        pool.wait_ge(pooled, n * NXB - (2 * NXB - b - 1))
                    nc.gpsimd.nop(nofuse=True)
                    for t in range(XB * b, XB * (b + 1)):
                        nc.gpsimd.indirect_dma_start(
                            out=x[:, slot, t, 0:EMB], out_offset=None, in_=t_table,
                            in_offset=bass.IndirectOffsetOnAxis(ap=idx[:, slot, t:t + 1], axis=0),
                        ).then_inc(x_in[slot][b], 16)

            gather(0, 0, True)
            gather(1, 0, True)
            with pool.Fori(1, BT) as m:
                gather(0, m, False)
                gather(1, m, False)

        @block.vector
        def _(dve):
            def scores(slot, m, ts):
                for t in ts:
                    if t == 0 and (not isinstance(m, int) or 2 * m + slot > 0):
                        dve.wait_ge(es_done, m * 2 + slot)
                    if t % XB == 0:
                        dve.wait_ge(x_in[slot][t // XB], (m + 1) * (16 * XB))
                    if t % 2 == 0 and (not isinstance(m, int) or 2 * m + slot > 0 or t > 0):
                        dve.wait_ge(score_step, (m * 2 + slot) * SCORE_STEPS + t // 2)
                    for head in range(2):
                        last = nc.vector.scalar_tensor_tensor(
                            junkv[:, 2 * (t % 2) + head, :], x[:, slot, t, 0:EMB], 1.0, wv[:, head, 0:EMB], ALU.mult, ALU.mult,
                            accum_out=score[:, head, t:t + 1])
                    if t % 2 or t == XT - 1:
                        last.then_inc(score_step, 1)

            def maxima(slot, m):
                n = m * 2 + slot
                dve.wait_ge(abs_done, (n + 1) * XT)
                nc.vector.tensor_scalar(iszero[:, :], absum[:, :], 0.0, None, ALU.is_equal).then_inc(att_step, 1)
                dve.wait_ge(att_step, n * ATT_STEPS + 1)
                dve.wait_ge(es_done, n + 1)
                nc.vector.nop(nofuse=True)
                for head in range(2):
                    last = nc.vector.copy_predicated(es[:, head, :], iszero[:, :], padrow[:, :])
                last.then_inc(att_step, 1)
                dve.wait_ge(att_step, n * ATT_STEPS + 2)
                nc.vector.reduce_max(mx[:, :], es[:, :, :], AX.X).then_inc(att_step, 1)
                dve.wait_ge(att_step, n * ATT_STEPS + 3)
                nc.vector.tensor_copy(mxo[0:HALF, :], mx[HALF:P, :])
                nc.vector.tensor_copy(mxo[HALF:P, :], mx[0:HALF, :]).then_inc(att_step, 1)
                dve.wait_ge(att_step, n * ATT_STEPS + 4)
                nc.vector.tensor_tensor(mxo[:, :], mx[:, :], mxo[:, :], ALU.max).then_inc(att_step, 1)
                dve.wait_ge(att_step, n * ATT_STEPS + 5)
                nc.vector.tensor_scalar(negmax[:, :], mxo[:, :], -1.0, None, ALU.mult).then_inc(att_step, 1)

            def reciprocal(slot, m):
                dve.wait_ge(pooled, m * (2 * NXB) + (slot + 1) * NXB)
                nc.vector.reciprocal(rsum[:, slot:slot + 1], ps[:, POOLED, EMB:XW]).then_inc(rsum_done, 1)

            def spread(slot, m, part):
                n = m * 2 + slot
                lo, hi = ((0, 13), (13, XT))[part]
                if part == 0:
                    dve.wait_ge(ew_done, n + 1)
                    if not isinstance(n, int) or n > 0:
                        dve.wait_ge(pooled, n * NXB)
                    else:
                        dve.wait_ge(g_step, 2)
                pv = pm[:, :].rearrange("p (t h b) -> p t h b", t=XT, h=2)[:, lo:hi, :, :]
                e = ew[:, :, lo:hi]
                ev = bass.AP(e.tensor, e.offset, [e.ap[0], [1, hi - lo], [XT, 2], [0, HALF]])
                sv = sel[:, :]
                sv = bass.AP(sv.tensor, sv.offset, [sv.ap[0], [0, hi - lo], [0, 2], [1, HALF]])
                nc.vector.tensor_tensor(pv, ev, sv, ALU.mult).then_inc(pm_done, 1)

            dve.wait_ge(v_in, 32)
            nc.vector.tensor_tensor(vi, vi, vj, ALU.mult).then_inc(g_step, 1)
            dve.wait_ge(g_step, 1)
            nc.vector.reduce_sum(gate[:, :], vi.rearrange("p (t c) -> p t c", c=RANK), AX.X).then_inc(g_step, 1)

            dve.wait_ge(wv_ready, 1)
            dve.wait_ge(init_done, 3)

            def attend(slot, m, first):
                scores(slot, m, range(XT))
                maxima(slot, m)
                if not first:
                    reciprocal(1 - slot, m if slot else m - 1)
                spread(slot, m, 0)
                spread(slot, m, 1)
            attend(0, 0, True)
            attend(1, 0, False)
            with dve.Fori(1, FIRST_HALVES // 2) as m:
                attend(0, m, False)
                attend(1, m, False)
            reciprocal(1, FIRST_HALVES // 2 - 1)

            units_before = [0]
            for s, nb in enumerate(SEGS):
                t0 = seg_start[s]
                dve.wait_ge(unit_ev, h_units[s])

                def products(it, pr, s=s, nb=nb, t0=t0):
                    sl = (2 * pr) % 4
                    k = 2 * pr
                    if s > 0 or not isinstance(it, int) or it > 0 or k >= 4:
                        dve.wait_ge(trans, (it + s * ITS) * KI + (k - 2))
                    if not isinstance(it, int) or it * KI + k < EMB:
                        hi = h2[:, t0, bass.ds(it * KI + k, 1)]
                        hj = h2[:, t0, bass.ds(it * KI + k + 1, 1)]
                        dst = cross[:, sl, 0, 0:1]
                        nc.vector.tensor_tensor(
                            bass.AP(dst.tensor, dst.offset, [dst.ap[0], [NBM * P, 2], [P, nb], [1, P]]),
                            bass.AP(hi.tensor, hi.offset, [hi.ap[0], [1, 2], [H2W, nb], [0, P]]),
                            bass.AP(hj.tensor, hj.offset, [hj.ap[0], [1, 2], [H2W, nb], [1, P]]),
                            ALU.mult).then_inc(prod, 1)
                        return
                    for a in range(2):
                        kt = it * KI + k + a
                        dst = cross[:, sl + a, 0, 0:1]
                        if kt < EMB + FAR_T:
                            i0 = FAR_I * (kt - EMB)
                            dims = ([P, nb], [FAR_D, FAR_I], [1, FAR_D])
                            idim = ([H2W, nb], [1, FAR_I], [0, FAR_D])
                            jdim = ([H2W, nb], [1, FAR_I], [1, FAR_D])
                            j0 = i0 + NEAR + 1
                        else:
                            i0 = OPP * (kt - EMB - FAR_T)
                            dims = ([P, nb], [1, OPP])
                            idim = jdim = ([H2W, nb], [1, OPP])
                            j0 = i0 + EMB // 2
                        hi = h2[:, t0, i0:i0 + 1]
                        hj = h2[:, t0, j0:j0 + 1]
                        last = nc.vector.tensor_tensor(
                            bass.AP(dst.tensor, dst.offset, [dst.ap[0], *dims]),
                            bass.AP(hi.tensor, hi.offset, [hi.ap[0], *idim]),
                            bass.AP(hj.tensor, hj.offset, [hj.ap[0], *jdim]), ALU.mult)
                    last.then_inc(prod, 1)

                def keys(tile, zstep, g, part):
                    if part == 0:
                        dve.wait_ge(le_in[g], (zstep + (tile * ZITS + 1)) * 16)
                    lo, hi = ((0, ZK // 2), (ZK // 2, ZK))[part]
                    for k in range(lo, hi):
                        last = nc.vector.scalar_tensor_tensor(
                            le[:, g, k, :], le[:, g, k, :], 1.0, out8[:, tile, :], ALU.mult, ALU.mult,
                            accum_out=zc[:, tile, bass.ds((zstep * UN + g) * ZK + k, 1)])
                    if part == 1:
                        last.then_inc(zdone, 1)

                def step(it, z, period):
                    for pr in range(KI // 2):
                        products(it, pr)
                        if z:
                            keys(z[0], z[1], pr // 2, pr % 2)
                        if period:
                            b, slot, m, kind = period
                            at = b * (KI // 2) + pr
                            if kind != "drain":
                                if at < 13:
                                    scores(slot, m, range(2 * at, min(2 * at + 2, XT)))
                                if at == 13:
                                    maxima(slot, m)
                            if at == 14 and kind != "first":
                                reciprocal(1 - slot, m if slot else m - 1)
                            if at >= 14 and kind != "drain":
                                spread(slot, m, at - 14)

                if s > 0:
                    dve.wait_ge(unit_ev, out8_units[s - 1])
                walk(dve, s, step, lambda tile: None)
            dve.wait_ge(unit_ev, out8_units[-1])
            for tile in seg_tiles[-1]:
                with dve.Fori(0, ZITS) as zstep:
                    for g in range(UN):
                        keys(tile, zstep, g, 0)
                        keys(tile, zstep, g, 1)

        @block.scalar
        def _(act):
            unit = counter()

            def absolutes(slot, m, ts):
                for t in ts:
                    if t % XB == 0:
                        act.wait_ge(x_in[slot][t // XB], (m + 1) * (16 * XB))
                    if t == 0 and (not isinstance(m, int) or 2 * m + slot > 0):
                        act.wait_ge(att_step, (m * 2 + slot) * ATT_STEPS - (ATT_STEPS - 1))
                    if not isinstance(m, int) or 2 * m + slot > 0 or t > 0:
                        act.wait_ge(abs_done, (m * 2 + slot) * XT + t)
                    nc.scalar.activation(junka[:, :], x[:, slot, t, 0:EMB], ACT.Abs,
                                         accum_out=absum[:, t:t + 1]).then_inc(abs_done, 1)

            def exp_scores(slot, m):
                n = m * 2 + slot
                act.wait_ge(score_step, (n + 1) * SCORE_STEPS)
                if not isinstance(n, int) or n > 0:
                    act.wait_ge(ew_done, n)
                for head in range(2):
                    last = nc.scalar.activation(es[:, head, :], score[:, head, :], ACT.Exp,
                                                bias=wv[:, head, EMB:XW])
                last.then_inc(es_done, 1)

            def exp_weights(slot, m):
                n = m * 2 + slot
                act.wait_ge(att_step, (n + 1) * ATT_STEPS)
                if not isinstance(n, int) or n > 0:
                    act.wait_ge(pm_done, n * 2)
                for head in range(2):
                    last = nc.scalar.activation(ew[:, head, :], es[:, head, :], ACT.Exp,
                                                bias=negmax[:, head:head + 1])
                last.then_inc(ew_done, 1)

            def normalise(slot, m):
                n = m * 2 + slot
                act.wait_ge(rsum_done, n + 1)
                nc.scalar.activation(q[:, bass.ds(n, 1), :].rearrange("p a e -> p (a e)"), ps[:, POOLED, 0:EMB],
                                     ACT.Copy, scale=rsum[:, slot:slot + 1]).then_inc(q_done, 1)

            def evacuate(u, outs):
                act.wait_ge(unit_mm, u + 1)
                for dst, src in outs:
                    last = nc.scalar.activation(dst, src, ACT.Copy)
                last.then_inc(unit_ev, 1)

            def bank(u):
                return MISC + u % 2

            def blocks(u, rows):
                return ps[0:rows, bank(u), 0:3 * P].rearrange("p (c b) -> p c b", c=3)

            def tails(tiles):
                for two in pairs(tiles):
                    for half in range(2):
                        for a, tile in enumerate(two):
                            u = unit()
                            dst = qT[:, a, :, :, half * HALF:(half + 1) * HALF]
                            evacuate(u, [(dst, ps[0:CH, bank(u), 0:3 * P].rearrange("p (c h b) -> p c h b", c=3, h=2))])
                    for a, tile in enumerate(two):
                        u = unit()
                        evacuate(u, [(h2[:, tile, 0:EMB], ps[:, bank(u), 0:EMB]),
                                     (h2[:, tile, EMB:H2W], ps[:, bank(u), 0:H2W - EMB])])
                    for a, tile in enumerate(two):
                        u = unit()
                        evacuate(u, [(hT[:, a, :, :], blocks(u, CH))])
                    for a, tile in enumerate(two):
                        u = unit()
                        evacuate(u, [(f6[:, a, :], ps[:, bank(u), 0:EMB])])
                    for a, tile in enumerate(two):
                        u = unit()
                        evacuate(u, [(f6T[:, tile, :, :], blocks(u, CH))])

            def finish(tiles):
                u = unit()
                evacuate(u, [(f7[:, b, :], ps[:, ACC + b, 0:EMB]) for b in range(len(tiles))])
                for two in pairs(list(enumerate(tiles))):
                    for a, (b, tile) in enumerate(two):
                        u = unit()
                        evacuate(u, [(f7T[:, a, :, :], blocks(u, CH))])
                    for a, (b, tile) in enumerate(two):
                        u = unit()
                        evacuate(u, [(out8[:, tile, :], ps[:, bank(u), 0:EMB])])

            def top(tile):
                u = unit()
                evacuate(u, [(zT, ps[0:108, bank(u), 0:2 * P].rearrange("p (c b) -> p c b", c=2))])
                for dst, b_, n in ((y1, bt1, HID1 // P), (y2, bt2, HID2 // P)):
                    u = unit()
                    act.wait_ge(unit_mm, u + 1)
                    for c in range(n):
                        last = nc.scalar.activation(dst[:, c, :], ps[:, bank(u), c * P:(c + 1) * P], ACT.Relu,
                                                    bias=b_[:, c:c + 1])
                    last.then_inc(unit_ev, 1)
                u = unit()
                evacuate(u, [(yrow[0:1, tile * P:(tile + 1) * P], ps[0:1, bank(u), 0:P])])

            act.wait_ge(wv_mm, 1)
            nc.scalar.activation(wv[:, :, :], ps[:, 0:2, 0:XW], ACT.Copy).then_inc(wv_ready, 1)
            act.wait_ge(wv_ready, 1)

            def attend(slot, m, first):
                absolutes(slot, m, range(XT))
                exp_scores(slot, m)
                exp_weights(slot, m)
                if not first:
                    normalise(1 - slot, m if slot else m - 1)
            attend(0, 0, True)
            attend(1, 0, False)
            with act.Fori(1, FIRST_HALVES // 2) as m:
                attend(0, m, False)
                attend(1, m, False)
            normalise(1, FIRST_HALVES // 2 - 1)
            act.wait_ge(const_in, 8 * 16)
            act.wait_ge(g_step, 2)

            for s, nb in enumerate(SEGS):
                if s == 0:
                    tails(seg_tiles[0])
                if s == 1:
                    tails([t for later in seg_tiles[1:] for t in later])

                def scale(it, k, s=s, nb=nb):
                    kt = it * KI + k
                    act.wait_ge(trans, kt + (s * KT + 1))
                    if s > 0 or not isinstance(it, int) or it > 0 or k >= 4:
                        act.wait_ge(summed, kt + (s * KT - 3))
                    nc.scalar.activation(crossT[:, k % 4, 0:nb, :].rearrange("p t b -> p (t b)"),
                                         ps[:, TBANK + k % 2, 0:nb * P], ACT.Copy,
                                         scale=gate[:, bass.ds(kt, 1)]).then_inc(scaled, 1)

                def step(it, z, period):
                    for k in range(KI):
                        scale(it, k)
                        if period:
                            b, slot, m, kind = period
                            at = b * KI + k
                            if kind != "drain":
                                if at < XT:
                                    absolutes(slot, m, [at])
                                if at == 25:
                                    exp_scores(slot, m)
                                if at == 27:
                                    exp_weights(slot, m)
                            if at == 29 and kind != "first":
                                normalise(1 - slot, m if slot else m - 1)

                walk(act, s, step, top)
                finish(seg_tiles[s])
            for tile in seg_tiles[-1]:
                top(tile)

        @block.tensor
        def _(pe):
            unit = counter()

            pe.wait_ge(att_in, 7 * 16)
            for head in range(2):
                last = nc.tensor.matmul(ps[:, head, 0:XW], w2rep[:, head, :], w1row[:, head, :],
                                        start=True, stop=True)
            last.then_inc(wv_mm, 1)

            def pool_rows(slot, m, ts):
                n = m * 2 + slot
                pmv = pm[:, :].rearrange("p (t m) -> p t m", t=XT)
                for t in ts:
                    if t == 0:
                        pe.wait_ge(pm_done, n * 2 + 2)
                        if not isinstance(n, int) or n > 0:
                            pe.wait_ge(q_done, n)
                    last = nc.tensor.matmul(ps[:, POOLED, 0:XW], pmv[:, t, :], x[:, slot, t, :],
                                            start=(t == 0), stop=(t == XT - 1))
                    if t % XB == XB - 1:
                        last.then_inc(pooled, 1)

            def bank(u):
                return MISC + u % 2

            def ready(u, back):
                need = u + 1 - min(back, 2)
                if need > 0:
                    pe.wait_ge(unit_ev, need)

            def transposes(u, src, rows):
                for c in range(3):
                    last = nc.tensor.transpose(ps[0:CH, bank(u), c * P:(c + 1) * P],
                                               src[:, c * CH:(c + 1) * CH], ident[:, :])
                last.then_inc(unit_mm, 1)

            def products(u, b_, terms):
                nc.tensor.matmul(ps[:, bank(u), 0:EMB], ones[:, :], bias[:, b_, :], start=True, stop=False)
                for a, (lhs, rhs) in enumerate(terms):
                    last = nc.tensor.matmul(ps[:, bank(u), 0:EMB], lhs, rhs, start=False, stop=(a == len(terms) - 1))
                last.then_inc(unit_mm, 1)

            def tails(tiles):
                pe.wait_ge(q_done, 2 * (tiles[-1] + 1))
                for two in pairs(tiles):
                    n = len(two)
                    for half in range(2):
                        for a, tile in enumerate(two):
                            u = unit()
                            ready(u, 2)
                            transposes(u, q[:, 2 * tile + half, :], CH)
                    for a, tile in enumerate(two):
                        u = unit()
                        ready(u, n)
                        products(u, 0, [(qT[:, a, c, head, :], w5[:, 3 * head + c, :])
                                        for head in range(2) for c in range(3)])
                    for a, tile in enumerate(two):
                        u = unit()
                        ready(u, n)
                        transposes(u, h2[:, tile, :], CH)
                    for a, tile in enumerate(two):
                        u = unit()
                        ready(u, n)
                        products(u, 1, [(hT[:, a, c, :], w6[:, c, :]) for c in range(3)])
                    for a, tile in enumerate(two):
                        u = unit()
                        ready(u, n)
                        transposes(u, f6[:, a, :], CH)

            def finish(tiles):
                unit()
                pe.drain().then_inc(unit_mm, 1)
                for two in pairs(list(enumerate(tiles))):
                    n = len(two)
                    for a, (b, tile) in enumerate(two):
                        u = unit()
                        ready(u, 1)
                        transposes(u, f7[:, b, :], CH)
                    for a, (b, tile) in enumerate(two):
                        u = unit()
                        ready(u, n)
                        products(u, 3, [(f6T[:, tile, c, :], w8[:, c, :]) for c in range(3)]
                                 + [(f7T[:, a, c, :], w8[:, 3 + c, :]) for c in range(3)])

            def top(tile):
                pe.wait_ge(zdone, (tile + 1) * ZITS * UN)
                pe.wait_ge(dense_in, 16)
                u = unit()
                ready(u, 2)
                for c in range(2):
                    last = nc.tensor.transpose(ps[0:108, bank(u), c * P:(c + 1) * P],
                                               zc[:, tile, c * 108:(c + 1) * 108], ident[:, :])
                last.then_inc(unit_mm, 1)
                for src, w, kn, mn in ((zT, wt1, 2, HID1 // P), (y1, wt2, HID1 // P, HID2 // P)):
                    u = unit()
                    ready(u, 1)
                    for m in range(mn):
                        for k in range(kn):
                            last = nc.tensor.matmul(ps[:, bank(u), m * P:(m + 1) * P], w[:, k, m * P:(m + 1) * P],
                                                    src[:, k, :], start=(k == 0), stop=(k == kn - 1))
                    last.then_inc(unit_mm, 1)
                u = unit()
                ready(u, 1)
                for k in range(HID2 // P):
                    last = nc.tensor.matmul(ps[0:1, bank(u), 0:P], wt3[:, k:k + 1], y2[:, k, :],
                                            start=(k == 0), stop=(k == HID2 // P - 1))
                last.then_inc(unit_mm, 1)

            pe.wait_ge(wv_ready, 1)
            pe.wait_ge(init_done, 3)
            pool_rows(0, 0, range(XT))
            pool_rows(1, 0, range(XT))
            with pe.Fori(1, FIRST_HALVES // 2) as m:
                pool_rows(0, m, range(XT))
                pool_rows(1, m, range(XT))
            pe.wait_ge(const_in, 8 * 16)

            for s, nb in enumerate(SEGS):
                if s == 0:
                    tails(seg_tiles[0])
                if s == 1:
                    tails([t for later in seg_tiles[1:] for t in later])

                def turn(it, k, s=s, nb=nb):
                    kt = it * KI + k
                    if k % 2 == 0:
                        pe.wait_ge(prod, it * (KI // 2) + (s * (KT // 2) + k // 2 + 1))
                    if s > 0 or not isinstance(it, int) or it > 0 or k >= 2:
                        pe.wait_ge(scaled, kt + (s * KT - 1))
                    for b in range(nb):
                        last = nc.tensor.transpose(ps[:, TBANK + k % 2, b * P:(b + 1) * P],
                                                   cross[:, k % 4, b, :], ident[:, :])
                    last.then_inc(trans, 1)

                def add(it, k, stop=False, s=s, nb=nb):
                    kt = it * KI + k
                    pe.wait_ge(scaled, kt + (s * KT + 1))
                    if k % GK == 0:
                        pe.wait_ge(w7_in[k // GK], (it + (s * ITS + 1)) * 16)
                    for b in range(nb):
                        last = nc.tensor.matmul(ps[:, ACC + b, 0:EMB], crossT[:, k % 4, b, :],
                                                w7[:, k // GK, k % GK, :], start=False, stop=stop)
                    last.then_inc(summed, 1)

                def step(it, z, period):
                    for k in range(KI):
                        end = isinstance(it, int) and it == ITS - 1 and k == KI - 1
                        if not end:
                            turn(it + (k + 1) // KI, (k + 1) % KI)
                        add(it, k, stop=end)
                        if period and period[3] != "first":
                            b, slot, m, kind = period
                            at = b * KI + k
                            if at < XT:
                                pool_rows(1 - slot, m if slot else m - 1, [at])

                for b in range(nb):
                    nc.tensor.matmul(ps[:, ACC + b, 0:EMB], ones[:, :], bias[:, 2, :], start=True, stop=False)
                turn(0, 0)
                walk(pe, s, step, top)
                finish(seg_tiles[s])
            for tile in seg_tiles[-1]:
                top(tile)


def _unit_counts():
    tail_units, top_units = 6, 4
    h, o8, n = [], [], 0
    for s, nb in enumerate(SEGS):
        if s == 0:
            n += tail_units * nb
        if s == 1:
            n += tail_units * (BT - SEGS[0])
        h.append(n)
        if s > 0:
            n += top_units * SEGS[s - 1]
        n += 1 + 2 * nb
        o8.append(n)
    n += top_units * SEGS[-1]
    return h, o8, n


h_units, out8_units, total_units = _unit_counts()


def kernel(**inputs):
    import concourse.bacc as _bacc
    from concourse.bass_utils import run_bass_kernel_spmd as _run

    a = {k: np.asarray(v) for k, v in inputs.items()}
    i, j, ok = pair_indices()
    lo, hi = np.minimum(i, j), np.maximum(i, j)
    row = lo * EMB - lo * (lo + 1) // 2 + (hi - lo - 1)
    w7 = a["L0_rec_w7"][np.where(ok, row, 0)]
    w7[~ok] = 0
    w7 = w7.reshape(GROUPS, GK, P, EMB).transpose(0, 2, 1, 3).reshape(GROUPS, P, GK * EMB)
    v = a["L0_rec_v"]

    def rows(index):
        r = v[index]
        r[~ok] = 0
        return r.transpose(1, 0, 2).reshape(P, KT * RANK)

    first = np.cumsum([0] + VOCAB[:-1])
    offs = first.reshape(XT, 2).T.repeat(HALF, axis=0)
    ids = a["ids"].reshape(2 * BT, HALF, XT, 2).transpose(3, 1, 0, 2).reshape(P, 2 * BT * XT)
    att = np.zeros((ATT, 2, P + XW), np.float32)
    for n, (wa, ba, wb) in enumerate((("w1", "b1", "w2"), ("w3", "b3", "w4"))):
        att[:, n, 0:P] = a["L0_rec_" + wb].reshape(ATT, 1)
        att[:, n, P:P + EMB] = a["L0_rec_" + wa].T
        att[:, n, P + EMB] = a["L0_rec_" + ba]
    arrays = {
        "table": np.concatenate([a[f"tbl_{n}"] for n in range(FEATS)], axis=0),
        "ids": ids, "offs": offs.astype(np.int32),
        "le": a["r_label_embedding"].reshape(BATCH, KEYS * EMB),
        "w7": w7, "vi": rows(i), "vj": rows(j), "att": att,
        "w5": a["L0_rec_w5"].reshape(6, CH, EMB).transpose(1, 0, 2),
        "w6": a["L0_rec_w6"].reshape(3, CH, EMB).transpose(1, 0, 2),
        "w8": a["L0_rec_w8"].reshape(6, CH, EMB).transpose(1, 0, 2),
        "bias": np.stack([a["L0_rec_b5"], a["L0_rec_b6"], a["L0_rec_b7"], a["L0_rec_b8"]])[None],
        "wt1": a["W_top1"].reshape(2, 108, HID1).transpose(1, 0, 2),
        "bt1": a["b_top1"].reshape(HID1 // P, P).T,
        "wt2": a["W_top2"].reshape(HID1 // P, P, HID2).transpose(1, 0, 2),
        "bt2": a["b_top2"].reshape(HID2 // P, P).T,
        "wt3": a["W_top3"].reshape(HID2 // P, P).T,
        "dense": a["dense_ctx"],
        "ident": np.eye(P, dtype=np.float32),
        "sel": np.tile(np.eye(HALF, dtype=np.float32), (2, 1)),
    }
    nc = _bacc.Bacc("TRN2", target_bir_lowering=False, num_devices=1)
    named, args = {}, []
    for name, arr in arrays.items():
        arr = np.ascontiguousarray(arr)
        named[f"in_{name}"] = arr
        args.append(nc.dram_tensor(f"in_{name}", arr.shape, mybir.dt.from_np(arr.dtype), kind="ExternalInput").ap())
    args.append(nc.dram_tensor("out_y", (1, BATCH), mybir.dt.float32, kind="ExternalOutput").ap())
    build(nc, *args)
    r = _run(nc, [named], core_ids=[0])
    return r.results[0]["out_y"].reshape(BATCH, 1)
```

```python
import concourse.bass as bass
import numpy as np
from concourse import mybir

BATCH, FEATS, EMB, KEYS = 1024, 50, 300, 200
DENSE, HID1, HID2, RANK, ATT = 16, 512, 256, 4, 8
VOCAB = [1250, 1250, 1250, 1000, 1250, 1250, 1000, 12500, 1000, 12500, 1250, 1000, 1250, 1000, 1250,
         1250, 1250, 1000, 12500, 12500, 1250, 12500, 1250, 1250, 1250, 12500, 1250, 1000, 1250, 1250,
         1000, 1250, 1000, 1000, 1000, 1000, 1250, 1250, 1250, 1000] + [1000] * 10
ROWS = sum(VOCAB)
PAD = float(np.float32(-2 ** 32 + 1))

P = 128
BT = BATCH // P
CH = EMB // 3
HALF = P // 2
XT = FEATS // 2
XB = 5
NXB = XT // XB
XW = EMB + 1

NEAR = P
FAR_D, FAR_I = EMB // 2 - 1 - NEAR, 6
FAR_T = EMB // FAR_I
OPP = EMB // 4
KT = EMB + FAR_T + 2
KI = 16
ITS = KT // KI
PR = KI // 2
WS = 4
MAIN_ITS = EMB // KI
H2W = EMB + EMB // 2

SEGS = [3, 3, 2]
NBM = max(SEGS)
ZK = 10
ZT = KEYS // ZK
ZN = 3

SPLIT = [(0, 2, 4, 6), (), ()]
ACT_PAIRS = [(), (), ()]

ACC, POOLED, TBANK, MISC = 0, 3, 4, 6


def pair_indices():
    i = np.zeros((KT, P), np.int64)
    j = np.zeros((KT, P), np.int64)
    ok = np.zeros((KT, P), bool)
    for t in range(EMB):
        i[t], j[t], ok[t] = t, (t + 1 + np.arange(P)) % EMB, True
    for m in range(FAR_T):
        for a in range(FAR_I):
            s = slice(FAR_D * a, FAR_D * (a + 1))
            i[EMB + m, s] = FAR_I * m + a
            j[EMB + m, s] = (FAR_I * m + a + NEAR + 1 + np.arange(FAR_D)) % EMB
            ok[EMB + m, s] = True
    for q in range(2):
        i[EMB + FAR_T + q, :OPP] = OPP * q + np.arange(OPP)
        j[EMB + FAR_T + q, :OPP] = OPP * q + np.arange(OPP) + EMB // 2
        ok[EMB + FAR_T + q, :OPP] = True
    return i, j, ok


def build(nc, t_table, t_ids, t_offs, t_le, t_w7, t_vi, t_vj, t_att, t_w5, t_w6, t_w8, t_bias,
          t_wt1, t_bt1, t_wt2, t_bt2, t_wt3, t_dense, t_ident, t_sel, out):
    f32, f32r, i32 = mybir.dt.float32, mybir.dt.float32r, mybir.dt.int32
    ALU, ACT, AX = mybir.AluOpType, mybir.ActivationFunctionType, mybir.AxisListType

    from contextlib import ExitStack
    ctx = ExitStack()
    with ctx:
        def sb(name, shape, dt=f32):
            return ctx.enter_context(nc.sbuf_tensor(name, shape, dt))

        def sem(name):
            return ctx.enter_context(nc.semaphore(name))

        ids = sb("ids", [P, BT * 2 * XT], i32)
        offs = sb("offs", [P, XT], i32)
        idx = sb("idx", [P, 2, XT], i32)
        big = sb("big", [P, 2 * XT * XW])
        x = big[:, :].rearrange("p (s t w) -> p s t w", s=2, t=XT)
        le = big[:, 0:ZN * ZK * EMB].rearrange("p (s k u) -> p s k u", s=ZN, k=ZK)
        zc = big[:, ZN * ZK * EMB:ZN * ZK * EMB + BT * (KEYS + DENSE)].rearrange("p (t k) -> p t k", t=BT)
        pm = sb("pm", [P, XT * 2 * HALF])
        vi = pm[:, 0:KT * RANK]
        vj = pm[:, KT * RANK:2 * KT * RANK]
        gate = sb("gate", [P, KT])
        ident = sb("ident", [P, P])
        sel = sb("sel", [P, HALF])
        ones = sb("ones", [1, P])
        wv = sb("wv", [P, 2, XW])
        score = sb("score", [P, 2, XT])
        absum = sb("absum", [P, XT])
        iszero = sb("iszero", [P, XT], i32)
        padrow = sb("padrow", [P, XT])
        es = sb("es", [P, 2, XT])
        ew = sb("ew", [P, 2, XT])
        mx = sb("mx", [P, 2])
        mxo = sb("mxo", [P, 2])
        negmax = sb("negmax", [P, 2])
        rsum = sb("rsum", [P, 2])
        junkv = sb("junkv", [P, 4, EMB])
        junka = sb("junka", [P, EMB])
        q = sb("q", [P, 2 * BT, EMB])
        qT = sb("qT", [CH, 2, 3, 2, P])
        h2 = sb("h2", [P, BT, H2W])
        hT = qT[:, :, :, 0, :]
        featT = qT[:, :, :, 1, :]
        out8 = q[:, :, :].rearrange("p (t a) e -> p a t e", a=2)[:, 0, :, :]
        f6 = q[:, :, :].rearrange("p (t a) e -> p a t e", a=2)[:, 1, :, :]
        f7 = f6[:, 0:NBM, :]
        w5 = sb("w5", [CH, 6, EMB])
        w6 = sb("w6", [CH, 3, EMB])
        w8 = sb("w8", [CH, 6, EMB])
        bias = sb("bias", [1, 4, EMB])
        cross = sb("cross", [P, 4, NBM, P])
        w2rep = cross[0:ATT, 0:2, 0, :]
        w1row = cross[0:ATT, 2:4, :, :].rearrange("p a t b -> p a (t b)")[:, :, 0:XW]
        crossT = sb("crossT", [P, 4, NBM, P])
        crossH = sb("crossH", [P, 4, NBM, P], f32r)
        crossL = sb("crossL", [P, 4, NBM, P], f32r)
        w7 = sb("w7", [P, WS, 2, EMB])
        w7H = sb("w7H", [P, WS, 2, EMB], f32r)
        w7L = sb("w7L", [P, WS, 2, EMB], f32r)
        wt1 = sb("wt1", [108, 2, HID1])
        bt1 = sb("bt1", [P, HID1 // P])
        wt2 = sb("wt2", [P, HID1 // P, HID2])
        bt2 = sb("bt2", [P, HID2 // P])
        wt3 = sb("wt3", [P, HID2 // P])
        y1 = pm[:, 0:HID1].rearrange("p (c b) -> p c b", b=P)
        y2 = pm[:, HID1:HID1 + HID2].rearrange("p (c b) -> p c b", b=P)
        zT = pm[0:108, HID1 + HID2:HID1 + HID2 + 2 * P].rearrange("p (c b) -> p c b", b=P)
        yrow = pm[0:1, 2 * BATCH:3 * BATCH]
        ps = ctx.enter_context(nc.psum_tensor("ps", [P, 8, 512], f32))

        att_in = sem("att_in")
        v_in = sem("v_in")
        const_in = sem("const_in")
        x_in = [[sem(f"x_in{s}_{b}") for b in range(NXB)] for s in range(2)]
        w7_in = [sem(f"w7_in{g}") for g in range(WS)]
        le_in = [sem(f"le_in{g}") for g in range(ZN)]
        dense_in = sem("dense_in")
        y_out = sem("y_out")
        idx_ready = sem("idx_ready")
        init_done = sem("init_done")
        wv_mm = sem("wv_mm")
        wv_ready = sem("wv_ready")
        g_step = sem("g_step")
        score_step = sem("score_step")
        abs_done = sem("abs_done")
        es_done = sem("es_done")
        att_step = sem("att_step")
        ew_done = sem("ew_done")
        pm_done = sem("pm_done")
        pooled = sem("pooled")
        rsum_done = sem("rsum_done")
        q_done = sem("q_done")
        prod = sem("prod")
        prod_act = sem("prod_act")
        high_w7 = sem("high_w7")
        low_w7 = sem("low_w7")
        low = sem("low")
        trans = sem("trans")
        scaled = sem("scaled")
        summed = sem("summed")
        zdone = sem("zdone")
        unit_mm = sem("unit_mm")
        unit_ev = sem("unit_ev")
        out8_done = sem("out8_done")

        ATT_STEPS = 6
        seg_start = [sum(SEGS[:s]) for s in range(len(SEGS))]
        seg_tiles = [list(range(a, a + n)) for a, n in zip(seg_start, SEGS)]
        FIRST_HALVES = 2 * SEGS[0]
        PRE = 3 + 4

        block = ctx.enter_context(nc.Block())

        def pairs(tiles):
            return [tiles[a:a + 2] for a in range(0, len(tiles), 2)]

        def counter():
            state = [0]

            def unit():
                state[0] += 1
                return state[0] - 1
            return unit

        def walk(eng, s, step, after):
            if s == 0:
                for it in (0, 1):
                    step(it, None, (it, FIRST_HALVES % 2, FIRST_HALVES // 2, "first"))
                with eng.Fori(0, 4) as r:
                    for a in range(2):
                        n = FIRST_HALVES + 1 + a
                        for b in range(2):
                            step(r * 4 + (2 + 2 * a + b), None, (b, n % 2, r + n // 2, "steady"))
                for it in (18, 19):
                    step(it, None, (it - 18, 1, BT - 1, "steady"))
                for it in (20, 21):
                    step(it, None, (it - 20, 0, BT, "drain"))
                return
            it = 0
            while it < ITS:
                end = it + 1
                while (not (s == 1 and it == 0) and end < MAIN_ITS and it < MAIN_ITS
                       and loads(s, it) == loads(s, end) and len(set(loads(s, it))) < 2
                       and end - 1 not in [due(s, tile) for tile in seg_tiles[s - 1]]):
                    end += 1
                if end - it > 1:
                    with eng.Fori(it, end) as i:
                        step(i, loads(s, it), None)
                else:
                    step(it, loads(s, it), None)
                for tile in seg_tiles[s - 1]:
                    if it <= due(s, tile) < end:
                        assert end - it == 1 or due(s, tile) == end - 1
                        after(tile)
                it = end

        def loads(s, it):
            tiles = seg_tiles[s - 1]
            return tuple(tiles[c // ZT] for c in range(ZN * it, ZN * it + ZN) if c < ZT * len(tiles))

        def due(s, tile):
            return min(((seg_tiles[s - 1].index(tile) + 1) * ZT - 1) // ZN + 1, ITS - 1)

        def scored_steps(eng, s, body):
            it = 0
            while loads(s, it):
                end = it + 1
                while (loads(s, it) == loads(s, end) and len(set(loads(s, it))) < 2
                       and not (s == 1 and it == 0)):
                    end += 1
                if end - it > 1:
                    with eng.Fori(it, end) as i:
                        for g, tile in enumerate(loads(s, it)):
                            body(i, g, tile)
                else:
                    for g, tile in enumerate(loads(s, it)):
                        body(it, g, tile)
                it = end

        ZSTEPS = [0] + [-(-ZT * n // ZN) for n in SEGS]
        zbase = [sum(ZSTEPS[:s + 1]) for s in range(len(SEGS) + 1)]

        def fast(s, k):
            return k // 2 in SPLIT[s]

        def loaded(it, pr, s):
            return (it * (PR // WS) + (s * ITS * (PR // WS) + pr // WS + 1)) * 16

        def low_count(s, it, k):
            before = sum(len(SPLIT[r]) * 2 * ITS for r in range(s))
            return it * (len(SPLIT[s]) * 2) + (before + sum(fast(s, n) for n in range(k + 1))
                                               - sum(fast(s, KI + n) for n in range(k + 1, 0)))

        def split_count(s, it, pr):
            before = sum(len(SPLIT[r]) * ITS for r in range(s))
            return it * len(SPLIT[s]) + (before + sum(n <= pr for n in SPLIT[s])
                                         - sum(n > pr + PR for n in SPLIT[s] if pr < 0))

        def prod_count(s, it, pr, on_act):
            own = [n for n in range(PR) if (n in ACT_PAIRS[s]) == on_act]
            end = PR if not on_act else 0
            before = 0
            for r in range(s):
                act_pairs = len(ACT_PAIRS[r]) * MAIN_ITS
                before += act_pairs if on_act else ITS * (PR) - act_pairs
            if isinstance(it, int) and it >= MAIN_ITS:
                return before + MAIN_ITS * len(own) + (it - MAIN_ITS) * end + (0 if on_act else pr + 1)
            return it * len(own) + (before + sum(n <= pr for n in own))

        def in_split(s, it, pr):
            return pr % PR in SPLIT[s] and not (pr >= PR and isinstance(it, int) and it == ITS - 1)

        def by_act(s, it, pr):
            return pr in ACT_PAIRS[s] and not (isinstance(it, int) and it >= MAIN_ITS)

        @block.sync
        def _(sp):
            for dst, src in ((ids[:, :], t_ids), (offs[:, :], t_offs), (w2rep, t_att[:, :, 0:P]),
                             (w1row, t_att[:, :, P:P + XW]), (sel[:, :], t_sel),
                             (ident[:, :], t_ident), (bias[:, :, :], t_bias)):
                sp.dma_start(dst, src).then_inc(att_in, 16)
            sp.dma_start(vi, t_vi).then_inc(v_in, 16)
            sp.dma_start(vj, t_vj).then_inc(v_in, 16)
            for dst, src in ((w5[:, :, :], t_w5), (w6[:, :, :], t_w6), (w8[:, :, :], t_w8),
                             (wt1[:, :, :], t_wt1), (bt1[:, :], t_bt1), (wt2[:, :, :], t_wt2),
                             (bt2[:, :], t_bt2), (wt3[:, :], t_wt3)):
                sp.dma_start(dst, src).then_inc(const_in, 16)

            for s, nb in enumerate(SEGS):
                def step(it, z, period, s=s):
                    for pr in range(PR):
                        if s > 0 or not isinstance(it, int) or it > 0 or pr >= WS:
                            last = pr - WS
                            if last % PR in SPLIT[s]:
                                sp.wait_ge(low_w7, split_count(s, it, last))
                                nc.sync.nop(nofuse=True)
                            if last % PR not in SPLIT[s] or last < 0 and last % PR not in SPLIT[s - 1]:
                                sp.wait_ge(summed, (it + s * ITS) * KI + 2 * (last + 1))
                        nc.sync.nop(nofuse=True)
                        sp.dma_start(w7[:, pr % WS, :, :].rearrange("p k u -> p (k u)"),
                                     t_w7[bass.ds(it * PR + pr, 1), :, :].rearrange("a p n -> (a p) n")
                                     ).then_inc(w7_in[pr % WS], 16)
                walk(sp, s, step, lambda tile: None)
            sp.wait_ge(unit_ev, total_units)
            sp.dma_start(out, yrow).then_inc(y_out, 16)
            sp.wait_ge(y_out, 16)

        @block.gpsimd
        def _(pool):
            nc.gpsimd.memset(ones[:, :], 1.0).then_inc(init_done, 1)
            nc.gpsimd.memset(padrow[:, :], PAD).then_inc(init_done, 1)
            nc.gpsimd.memset(x[:, :, :, EMB:XW], 1.0).then_inc(init_done, 1)
            pool.wait_ge(att_in, 7 * 16)

            def gather(slot, m, first):
                n = m * 2 + slot
                if not first:
                    pool.wait_ge(pooled, n * NXB - (2 * NXB - 1))
                nc.gpsimd.tensor_tensor(idx[:, slot, :], ids[:, bass.ds(n * XT, XT)], offs[:, :],
                                        ALU.add).then_inc(idx_ready, 1)
                pool.wait_ge(idx_ready, n + 1)
                for b in range(NXB):
                    if not first and b:
                        pool.wait_ge(pooled, n * NXB - (2 * NXB - b - 1))
                    nc.gpsimd.nop(nofuse=True)
                    for t in range(XB * b, XB * (b + 1)):
                        nc.gpsimd.indirect_dma_start(
                            out=x[:, slot, t, 0:EMB], out_offset=None, in_=t_table,
                            in_offset=bass.IndirectOffsetOnAxis(ap=idx[:, slot, t:t + 1], axis=0),
                        ).then_inc(x_in[slot][b], 16)

            gather(0, 0, True)
            gather(1, 0, True)
            with pool.Fori(1, BT) as m:
                gather(0, m, False)
                gather(1, m, False)

            def load_le(s, it, g, tile):
                step_no = it + zbase[s - 1]
                if isinstance(step_no, int) and step_no == 0:
                    if g == 0:
                        pool.wait_ge(pooled, 2 * BT * NXB)
                        pool.dma_start(zc[:, :, KEYS:], t_dense.rearrange("(t p) c -> p t c", p=P)
                                     ).then_inc(dense_in, 16)
                else:
                    pool.wait_ge(zdone, step_no * ZN + (g + 1 - ZN))
                key = (it * ZN + (g - ZT * seg_tiles[s - 1].index(tile))) * (ZK * EMB)
                rows = t_le[tile * P:(tile + 1) * P, bass.ds(key, ZK * EMB)]
                pool.dma_start(le[:, g, :, :].rearrange("p k u -> p (k u)"), rows).then_inc(le_in[g], 16)

            for s in range(1, len(SEGS) + 1):
                scored_steps(pool, s, lambda it, g, tile, s=s: load_le(s, it, g, tile))

        @block.vector
        def _(dve):
            def scores(slot, m, ts):
                for t in ts:
                    if t == 0 and (not isinstance(m, int) or 2 * m + slot > 0):
                        dve.wait_ge(es_done, m * 2 + slot)
                    if t % XB == 0:
                        dve.wait_ge(x_in[slot][t // XB], (m + 1) * (16 * XB))
                    if not isinstance(m, int) or 2 * m + slot > 0 or t > 1:
                        dve.wait_ge(score_step, (m * 2 + slot) * XT + (t - 1))
                    for head in range(2):
                        last = nc.vector.scalar_tensor_tensor(
                            junkv[:, 2 * ((t + slot) % 2) + head, :], x[:, slot, t, 0:EMB], 1.0,
                            wv[:, head, 0:EMB], ALU.mult, ALU.mult, accum_out=score[:, head, t:t + 1])
                    last.then_inc(score_step, 1)

            def maxima(slot, m):
                n = m * 2 + slot
                dve.wait_ge(abs_done, (n + 1) * XT)
                nc.vector.tensor_scalar(iszero[:, :], absum[:, :], 0.0, None, ALU.is_equal).then_inc(att_step, 1)
                dve.wait_ge(att_step, n * ATT_STEPS + 1)
                dve.wait_ge(es_done, n + 1)
                nc.vector.nop(nofuse=True)
                for head in range(2):
                    last = nc.vector.copy_predicated(es[:, head, :], iszero[:, :], padrow[:, :])
                last.then_inc(att_step, 1)
                dve.wait_ge(att_step, n * ATT_STEPS + 2)
                nc.vector.reduce_max(mx[:, :], es[:, :, :], AX.X).then_inc(att_step, 1)
                dve.wait_ge(att_step, n * ATT_STEPS + 3)
                nc.vector.tensor_copy(mxo[0:HALF, :], mx[HALF:P, :])
                nc.vector.tensor_copy(mxo[HALF:P, :], mx[0:HALF, :]).then_inc(att_step, 1)
                dve.wait_ge(att_step, n * ATT_STEPS + 4)
                nc.vector.tensor_tensor(mxo[:, :], mx[:, :], mxo[:, :], ALU.max).then_inc(att_step, 1)
                dve.wait_ge(att_step, n * ATT_STEPS + 5)
                nc.vector.tensor_scalar(negmax[:, :], mxo[:, :], -1.0, None, ALU.mult).then_inc(att_step, 1)

            def reciprocal(slot, m):
                dve.wait_ge(pooled, m * (2 * NXB) + (slot + 1) * NXB)
                nc.vector.reciprocal(rsum[:, slot:slot + 1], ps[:, POOLED, EMB:XW]).then_inc(rsum_done, 1)

            def spread(slot, m, part):
                n = m * 2 + slot
                lo, hi = ((0, 7), (7, 13), (13, 19), (19, XT))[part]
                if part == 0:
                    dve.wait_ge(ew_done, n + 1)
                    if not isinstance(n, int) or n > 0:
                        dve.wait_ge(pooled, n * NXB)
                    else:
                        dve.wait_ge(g_step, 2)
                pv = pm[:, :].rearrange("p (t h b) -> p t h b", t=XT, h=2)[:, lo:hi, :, :]
                e = ew[:, :, lo:hi]
                ev = bass.AP(e.tensor, e.offset, [e.ap[0], [1, hi - lo], [XT, 2], [0, HALF]])
                sv = sel[:, :]
                sv = bass.AP(sv.tensor, sv.offset, [sv.ap[0], [0, hi - lo], [0, 2], [1, HALF]])
                nc.vector.tensor_tensor(pv, ev, sv, ALU.mult).then_inc(pm_done, 1)

            dve.wait_ge(v_in, 32)
            nc.vector.tensor_tensor(vi, vi, vj, ALU.mult).then_inc(g_step, 1)
            dve.wait_ge(g_step, 1)
            nc.vector.reduce_sum(gate[:, :], vi.rearrange("p (t c) -> p t c", c=RANK), AX.X).then_inc(g_step, 1)

            dve.wait_ge(wv_ready, 1)
            dve.wait_ge(init_done, 3)

            def attend(slot, m, first):
                scores(slot, m, range(XT))
                maxima(slot, m)
                if not first:
                    reciprocal(1 - slot, m if slot else m - 1)
                for part in range(4):
                    spread(slot, m, part)
            attend(0, 0, True)
            attend(1, 0, False)
            with dve.Fori(1, FIRST_HALVES // 2) as m:
                attend(0, m, False)
                attend(1, m, False)
            reciprocal(1, FIRST_HALVES // 2 - 1)

            def key_scores(s, it, g, tile, part):
                lo, hi = part
                if lo == 0:
                    dve.wait_ge(le_in[g], (it + (zbase[s - 1] + 1)) * 16)
                for k in range(lo, hi):
                    key = (it * ZN + (g - ZT * seg_tiles[s - 1].index(tile))) * ZK + k
                    last = nc.vector.scalar_tensor_tensor(
                        le[:, g, k, :], le[:, g, k, :], 1.0, out8[:, tile, :], ALU.mult, ALU.mult,
                        accum_out=zc[:, tile, bass.ds(key, 1)])
                if hi == ZK:
                    last.then_inc(zdone, 1)

            for s, nb in enumerate(SEGS):
                t0 = seg_start[s]
                dve.wait_ge(unit_ev, h_units[s])

                def products(it, pr, s=s, nb=nb, t0=t0):
                    sl = (2 * pr) % 4
                    k = 2 * pr
                    if s > 0 or not isinstance(it, int) or it > 0 or k >= 4:
                        dve.wait_ge(trans, (it + s * ITS) * KI + (k - 2))
                    if not isinstance(it, int) or it * KI + k < EMB:
                        hi = h2[:, t0, bass.ds(it * KI + k, 1)]
                        hj = h2[:, t0, bass.ds(it * KI + k + 1, 1)]
                        dst = cross[:, sl, 0, 0:1]
                        nc.vector.tensor_tensor(
                            bass.AP(dst.tensor, dst.offset, [dst.ap[0], [NBM * P, 2], [P, nb], [1, P]]),
                            bass.AP(hi.tensor, hi.offset, [hi.ap[0], [1, 2], [H2W, nb], [0, P]]),
                            bass.AP(hj.tensor, hj.offset, [hj.ap[0], [1, 2], [H2W, nb], [1, P]]),
                            ALU.mult).then_inc(prod, 1)
                        return
                    for a in range(2):
                        kt = it * KI + k + a
                        dst = cross[:, sl + a, 0, 0:1]
                        if kt < EMB + FAR_T:
                            i0 = FAR_I * (kt - EMB)
                            dims = ([P, nb], [FAR_D, FAR_I], [1, FAR_D])
                            idim = ([H2W, nb], [1, FAR_I], [0, FAR_D])
                            jdim = ([H2W, nb], [1, FAR_I], [1, FAR_D])
                            j0 = i0 + NEAR + 1
                        else:
                            i0 = OPP * (kt - EMB - FAR_T)
                            dims = ([P, nb], [1, OPP])
                            idim = jdim = ([H2W, nb], [1, OPP])
                            j0 = i0 + EMB // 2
                        hi = h2[:, t0, i0:i0 + 1]
                        hj = h2[:, t0, j0:j0 + 1]
                        last = nc.vector.tensor_tensor(
                            bass.AP(dst.tensor, dst.offset, [dst.ap[0], *dims]),
                            bass.AP(hi.tensor, hi.offset, [hi.ap[0], *idim]),
                            bass.AP(hj.tensor, hj.offset, [hj.ap[0], *jdim]), ALU.mult)
                    last.then_inc(prod, 1)

                def low_part(it, k, s=s, nb=nb):
                    kt = it * KI + k
                    dve.wait_ge(scaled, kt + (s * KT + 1))
                    nc.vector.scalar_tensor_tensor(
                        crossL[:, k % 4, 0:nb, :].rearrange("p t b -> p (t b)"),
                        ps[:, TBANK + k % 2, 0:nb * P], gate[:, bass.ds(kt, 1)],
                        crossH[:, k % 4, 0:nb, :].rearrange("p t b -> p (t b)").bitcast(f32),
                        ALU.mult, ALU.subtract).then_inc(low, 1)

                def low_weights(it, pr, s=s):
                    dve.wait_ge(high_w7, split_count(s, it, pr))
                    nc.vector.tensor_tensor(w7L[:, pr % WS, :, :], w7[:, pr % WS, :, :],
                                            w7H[:, pr % WS, :, :].bitcast(f32), ALU.subtract).then_inc(low_w7, 1)

                def step(it, z, period, s=s):
                    for k in range(KI):
                        if k % 2 == 0:
                            ahead, pr = (k + 4) // KI, (k + 4) % KI // 2
                            if not (isinstance(it, int) and it + ahead == ITS) and not by_act(s, it + ahead, pr):
                                products(it + ahead, pr)
                        if fast(s, k):
                            low_part(it, k)
                        if k % 2 and in_split(s, it, (k + 3) // 2):
                            low_weights(it + (k + 3) // KI, (k + 3) // 2 % PR)
                        if z and k // 4 < len(z):
                            key_scores(s, it, k // 4, z[k // 4], ((0, 3), (3, 5), (5, 8), (8, ZK))[k % 4])
                        if period:
                            b, slot, m, kind = period
                            at = b * KI + k
                            if kind != "drain":
                                if at < XT:
                                    scores(slot, m, [at])
                                if at == 26:
                                    maxima(slot, m)
                            if at == 28 and kind != "first":
                                reciprocal(1 - slot, m if slot else m - 1)
                            if at >= 28 and kind != "drain":
                                spread(slot, m, at - 28)

                products(0, 0)
                products(0, 1)
                for pr in (0, 1):
                    if pr in SPLIT[s]:
                        low_weights(0, pr)
                if s > 0:
                    dve.wait_ge(out8_done, sum(SEGS[:s]))
                walk(dve, s, step, lambda tile: None)
                for b, tile in enumerate(seg_tiles[s]):
                    u = out8_units[s][b]
                    dve.wait_ge(unit_mm, u + 1)
                    nc.vector.tensor_tensor(out8[:, tile, :], ps[:, MISC + u % 2, 0:EMB], out8[:, tile, :],
                                            ALU.add).then_inc(out8_done, 1)
            dve.wait_ge(out8_done, BT)
            scored_steps(dve, len(SEGS), lambda it, g, tile: key_scores(len(SEGS), it, g, tile, (0, ZK)))

        @block.scalar
        def _(act):
            unit = counter()

            def absolutes(slot, m, ts):
                for t in ts:
                    if t % XB == 0:
                        act.wait_ge(x_in[slot][t // XB], (m + 1) * (16 * XB))
                    if t == 0 and (not isinstance(m, int) or 2 * m + slot > 0):
                        act.wait_ge(att_step, (m * 2 + slot) * ATT_STEPS - (ATT_STEPS - 1))
                    if not isinstance(m, int) or 2 * m + slot > 0 or t > 0:
                        act.wait_ge(abs_done, (m * 2 + slot) * XT + t)
                    nc.scalar.activation(junka[:, :], x[:, slot, t, 0:EMB], ACT.Abs,
                                         accum_out=absum[:, t:t + 1]).then_inc(abs_done, 1)

            def exp_scores(slot, m):
                n = m * 2 + slot
                act.wait_ge(score_step, (n + 1) * XT)
                if not isinstance(n, int) or n > 0:
                    act.wait_ge(ew_done, n)
                for head in range(2):
                    last = nc.scalar.activation(es[:, head, :], score[:, head, :], ACT.Exp,
                                                bias=wv[:, head, EMB:XW])
                last.then_inc(es_done, 1)

            def exp_weights(slot, m):
                n = m * 2 + slot
                act.wait_ge(att_step, (n + 1) * ATT_STEPS)
                if not isinstance(n, int) or n > 0:
                    act.wait_ge(pm_done, n * 4)
                for head in range(2):
                    last = nc.scalar.activation(ew[:, head, :], es[:, head, :], ACT.Exp,
                                                bias=negmax[:, head:head + 1])
                last.then_inc(ew_done, 1)

            def normalise(slot, m):
                n = m * 2 + slot
                act.wait_ge(rsum_done, n + 1)
                nc.scalar.activation(q[:, bass.ds(n, 1), :].rearrange("p a e -> p (a e)"), ps[:, POOLED, 0:EMB],
                                     ACT.Copy, scale=rsum[:, slot:slot + 1]).then_inc(q_done, 1)

            def evacuate(u, outs):
                act.wait_ge(unit_mm, u + 1)
                for dst, src in outs:
                    last = nc.scalar.activation(dst, src, ACT.Copy)
                last.then_inc(unit_ev, 1)

            def bank(u):
                return MISC + u % 2

            def blocks(u, rows):
                return ps[0:rows, bank(u), 0:3 * P].rearrange("p (c b) -> p c b", c=3)

            def tails(tiles):
                for two in pairs(tiles):
                    for half in range(2):
                        for a, tile in enumerate(two):
                            u = unit()
                            dst = qT[:, a, :, :, half * HALF:(half + 1) * HALF]
                            evacuate(u, [(dst, ps[0:CH, bank(u), 0:3 * P].rearrange("p (c h b) -> p c h b", c=3, h=2))])
                    for a, tile in enumerate(two):
                        u = unit()
                        evacuate(u, [(h2[:, tile, 0:EMB], ps[:, bank(u), 0:EMB]),
                                     (h2[:, tile, EMB:H2W], ps[:, bank(u), 0:H2W - EMB])])
                    for a, tile in enumerate(two):
                        u = unit()
                        evacuate(u, [(hT[:, a, :, :], blocks(u, CH))])
                    for a, tile in enumerate(two):
                        u = unit()
                        evacuate(u, [(f6[:, tile, :], ps[:, bank(u), 0:EMB])])
                    for a, tile in enumerate(two):
                        u = unit()
                        evacuate(u, [(featT[:, a, :, :], blocks(u, CH))])
                    for a, tile in enumerate(two):
                        u = unit()
                        evacuate(u, [(out8[:, tile, :], ps[:, bank(u), 0:EMB])])

            def finish(tiles):
                u = unit()
                evacuate(u, [(f7[:, b, :], ps[:, ACC + b, 0:EMB]) for b in range(len(tiles))])
                for two in pairs(list(enumerate(tiles))):
                    for a, (b, tile) in enumerate(two):
                        u = unit()
                        evacuate(u, [(featT[:, a, :, :], blocks(u, CH))])
                    for a, (b, tile) in enumerate(two):
                        unit()
                        act.wait_ge(out8_done, tile + 1)
                        act.drain().then_inc(unit_ev, 1)

            def top(tile):
                u = unit()
                evacuate(u, [(zT, ps[0:108, bank(u), 0:2 * P].rearrange("p (c b) -> p c b", c=2))])
                for dst, b_, n in ((y1, bt1, HID1 // P), (y2, bt2, HID2 // P)):
                    u = unit()
                    act.wait_ge(unit_mm, u + 1)
                    for c in range(n):
                        last = nc.scalar.activation(dst[:, c, :], ps[:, bank(u), c * P:(c + 1) * P], ACT.Relu,
                                                    bias=b_[:, c:c + 1])
                    last.then_inc(unit_ev, 1)
                u = unit()
                evacuate(u, [(yrow[0:1, tile * P:(tile + 1) * P], ps[0:1, bank(u), 0:P])])

            act.wait_ge(wv_mm, 1)
            nc.scalar.activation(wv[:, :, :], ps[:, 0:2, 0:XW], ACT.Copy).then_inc(wv_ready, 1)
            act.wait_ge(wv_ready, 1)

            def attend(slot, m, first):
                absolutes(slot, m, range(XT))
                exp_scores(slot, m)
                exp_weights(slot, m)
                if not first:
                    normalise(1 - slot, m if slot else m - 1)
            attend(0, 0, True)
            attend(1, 0, False)
            with act.Fori(1, FIRST_HALVES // 2) as m:
                attend(0, m, False)
                attend(1, m, False)
            normalise(1, FIRST_HALVES // 2 - 1)
            act.wait_ge(const_in, 8 * 16)
            act.wait_ge(g_step, 2)

            for s, nb in enumerate(SEGS):
                if s == 0:
                    tails(seg_tiles[0])
                if s == 1:
                    tails([t for later in seg_tiles[1:] for t in later])

                def scale(it, k, s=s, nb=nb):
                    kt = it * KI + k
                    act.wait_ge(trans, kt + (s * KT + 1))
                    if s > 0 or not isinstance(it, int) or it > 0 or k >= 4:
                        act.wait_ge(summed, kt + (s * KT - 3))
                    dst = crossH if fast(s, k) else crossT
                    nc.scalar.activation(dst[:, k % 4, 0:nb, :].rearrange("p t b -> p (t b)"),
                                         ps[:, TBANK + k % 2, 0:nb * P], ACT.Copy,
                                         scale=gate[:, bass.ds(kt, 1)]).then_inc(scaled, 1)

                def high_weights(it, pr, s=s):
                    act.wait_ge(w7_in[pr % WS], loaded(it, pr, s))
                    if s > 0 or not isinstance(it, int) or it > 0 or pr >= WS:
                        act.wait_ge(summed, it * KI + (s * KT + 2 * (pr - WS + 1)))
                    nc.scalar.activation(w7H[:, pr % WS, :, :], w7[:, pr % WS, :, :], ACT.Copy).then_inc(high_w7, 1)

                def products(it, pr, s=s, nb=nb, t0=seg_start[s]):
                    act.wait_ge(trans, it * KI + (s * KT + 2 * pr - 2))
                    for k in (2 * pr, 2 * pr + 1):
                        for b in range(nb):
                            last = nc.scalar.activation(
                                cross[:, k % 4, b, :], h2[:, t0 + b, bass.ds(it * KI + (k + 1), P)], ACT.Copy,
                                scale=h2[:, t0 + b, bass.ds(it * KI + k, 1)])
                    last.then_inc(prod_act, 1)

                def step(it, z, period, s=s):
                    for k in range(KI):
                        scale(it, k)
                        if k % 2 == 0 and in_split(s, it, (k + 4) // 2):
                            high_weights(it + (k + 4) // KI, (k + 4) // 2 % PR)
                        if k % 2 == 1 and k + 3 < KI and by_act(s, it, (k + 3) // 2):
                            products(it, (k + 3) // 2)
                        if period:
                            b, slot, m, kind = period
                            at = b * KI + k
                            if kind != "drain":
                                if at < XT:
                                    absolutes(slot, m, [at])
                                if at == 25:
                                    exp_scores(slot, m)
                                if at == 27:
                                    exp_weights(slot, m)
                            if at == 29 and kind != "first":
                                normalise(1 - slot, m if slot else m - 1)

                for pr in (0, 1):
                    if pr in SPLIT[s]:
                        high_weights(0, pr)
                walk(act, s, step, top)
                finish(seg_tiles[s])
            for tile in seg_tiles[-1]:
                top(tile)

        @block.tensor
        def _(pe):
            unit = counter()

            pe.wait_ge(att_in, 7 * 16)
            for head in range(2):
                last = nc.tensor.matmul(ps[:, head, 0:XW], w2rep[:, head, :], w1row[:, head, :],
                                        start=True, stop=True)
            last.then_inc(wv_mm, 1)

            def pool_rows(slot, m, ts):
                n = m * 2 + slot
                pmv = pm[:, :].rearrange("p (t m) -> p t m", t=XT)
                for t in ts:
                    if t == 0:
                        pe.wait_ge(pm_done, n * 4 + 4)
                        if not isinstance(n, int) or n > 0:
                            pe.wait_ge(q_done, n)
                    last = nc.tensor.matmul(ps[:, POOLED, 0:XW], pmv[:, t, :], x[:, slot, t, :],
                                            start=(t == 0), stop=(t == XT - 1))
                    if t % XB == XB - 1:
                        last.then_inc(pooled, 1)

            def bank(u):
                return MISC + u % 2

            def ready(u, back):
                need = u + 1 - min(back, 2)
                if need > 0:
                    pe.wait_ge(unit_ev, need)

            def transposes(u, src, rows):
                for c in range(3):
                    last = nc.tensor.transpose(ps[0:CH, bank(u), c * P:(c + 1) * P],
                                               src[:, c * CH:(c + 1) * CH], ident[:, :])
                last.then_inc(unit_mm, 1)

            def products(u, b_, terms):
                if b_ is not None:
                    nc.tensor.matmul(ps[:, bank(u), 0:EMB], ones[:, :], bias[:, b_, :], start=True, stop=False)
                for a, (lhs, rhs) in enumerate(terms):
                    last = nc.tensor.matmul(ps[:, bank(u), 0:EMB], lhs, rhs, start=(b_ is None and a == 0),
                                            stop=(a == len(terms) - 1))
                last.then_inc(unit_mm, 1)

            def tails(tiles):
                pe.wait_ge(q_done, 2 * (tiles[-1] + 1))
                for two in pairs(tiles):
                    n = len(two)
                    for half in range(2):
                        for a, tile in enumerate(two):
                            u = unit()
                            ready(u, 2)
                            transposes(u, q[:, 2 * tile + half, :], CH)
                    for a, tile in enumerate(two):
                        u = unit()
                        ready(u, n)
                        products(u, 0, [(qT[:, a, c, head, :], w5[:, 3 * head + c, :])
                                        for head in range(2) for c in range(3)])
                    for a, tile in enumerate(two):
                        u = unit()
                        ready(u, n)
                        transposes(u, h2[:, tile, :], CH)
                    for a, tile in enumerate(two):
                        u = unit()
                        ready(u, n)
                        products(u, 1, [(hT[:, a, c, :], w6[:, c, :]) for c in range(3)])
                    for a, tile in enumerate(two):
                        u = unit()
                        ready(u, n)
                        transposes(u, f6[:, tile, :], CH)
                    for a, tile in enumerate(two):
                        u = unit()
                        ready(u, n)
                        products(u, 3, [(featT[:, a, c, :], w8[:, c, :]) for c in range(3)])

            def finish(tiles):
                unit()
                pe.drain().then_inc(unit_mm, 1)
                for two in pairs(list(enumerate(tiles))):
                    n = len(two)
                    for a, (b, tile) in enumerate(two):
                        u = unit()
                        ready(u, 1)
                        transposes(u, f7[:, b, :], CH)
                    for a, (b, tile) in enumerate(two):
                        u = unit()
                        ready(u, n)
                        products(u, None, [(featT[:, a, c, :], w8[:, 3 + c, :]) for c in range(3)])

            def top(tile):
                pe.wait_ge(zdone, (tile + 1) * ZT)
                pe.wait_ge(dense_in, 16)
                u = unit()
                ready(u, 2)
                for c in range(2):
                    last = nc.tensor.transpose(ps[0:108, bank(u), c * P:(c + 1) * P],
                                               zc[:, tile, c * 108:(c + 1) * 108], ident[:, :])
                last.then_inc(unit_mm, 1)
                for src, w, kn, mn in ((zT, wt1, 2, HID1 // P), (y1, wt2, HID1 // P, HID2 // P)):
                    u = unit()
                    ready(u, 1)
                    for m in range(mn):
                        for k in range(kn):
                            last = nc.tensor.matmul(ps[:, bank(u), m * P:(m + 1) * P], w[:, k, m * P:(m + 1) * P],
                                                    src[:, k, :], start=(k == 0), stop=(k == kn - 1))
                    last.then_inc(unit_mm, 1)
                u = unit()
                ready(u, 1)
                for k in range(HID2 // P):
                    last = nc.tensor.matmul(ps[0:1, bank(u), 0:P], wt3[:, k:k + 1], y2[:, k, :],
                                            start=(k == 0), stop=(k == HID2 // P - 1))
                last.then_inc(unit_mm, 1)

            pe.wait_ge(wv_ready, 1)
            pe.wait_ge(init_done, 3)
            pool_rows(0, 0, range(XT))
            pool_rows(1, 0, range(XT))
            with pe.Fori(1, FIRST_HALVES // 2) as m:
                pool_rows(0, m, range(XT))
                pool_rows(1, m, range(XT))
            pe.wait_ge(const_in, 8 * 16)

            for s, nb in enumerate(SEGS):
                if s == 0:
                    tails(seg_tiles[0])
                if s == 1:
                    tails([t for later in seg_tiles[1:] for t in later])

                def turn(it, k, s=s, nb=nb):
                    kt = it * KI + k
                    if k % 2 == 0:
                        if by_act(s, it, k // 2):
                            pe.wait_ge(prod_act, prod_count(s, it, k // 2, True))
                        else:
                            pe.wait_ge(prod, prod_count(s, it, k // 2, False))
                    if s > 0 or not isinstance(it, int) or it > 0 or k >= 2:
                        pe.wait_ge(scaled, kt + (s * KT - 1))
                        if fast(s, (k - 2) % KI):
                            pe.wait_ge(low, low_count(s, it, k - 2))
                    for b in range(nb):
                        last = nc.tensor.transpose(ps[:, TBANK + k % 2, b * P:(b + 1) * P],
                                                   cross[:, k % 4, b, :], ident[:, :])
                    last.then_inc(trans, 1)

                def add(it, k, stop=False, s=s, nb=nb):
                    kt = it * KI + k
                    if fast(s, k):
                        pe.wait_ge(low, low_count(s, it, k))
                        if k % 2 == 0:
                            pe.wait_ge(low_w7, split_count(s, it, k // 2))
                        wh, wl = (w[:, k // 2 % WS, k % 2, :] for w in (w7H, w7L))
                        for b in range(nb):
                            hi, lo = crossH[:, k % 4, b, :], crossL[:, k % 4, b, :]
                            for lhs, rhs, end in ((hi, wh, False), (hi, wl, False), (lo, wh, True)):
                                last = nc.tensor.matmul(ps[:, ACC + b, 0:EMB], lhs, rhs, start=False,
                                                        stop=(stop and end))
                    else:
                        pe.wait_ge(scaled, kt + (s * KT + 1))
                        if k % 2 == 0:
                            pe.wait_ge(w7_in[k // 2 % WS], loaded(it, k // 2, s))
                        for b in range(nb):
                            last = nc.tensor.matmul(ps[:, ACC + b, 0:EMB], crossT[:, k % 4, b, :],
                                                    w7[:, k // 2 % WS, k % 2, :], start=False, stop=stop)
                    last.then_inc(summed, 1)

                def step(it, z, period, s=s):
                    for k in range(KI):
                        last_it = isinstance(it, int) and it == ITS - 1
                        if not (last_it and k >= KI - 2):
                            turn(it + (k + 2) // KI, (k + 2) % KI)
                        add(it, k, stop=(last_it and k == KI - 1))
                        if period and period[3] != "first":
                            b, slot, m, kind = period
                            at = b * KI + k
                            if at < XT:
                                pool_rows(1 - slot, m if slot else m - 1, [at])

                for b in range(nb):
                    nc.tensor.matmul(ps[:, ACC + b, 0:EMB], ones[:, :], bias[:, 2, :], start=True, stop=False)
                turn(0, 0)
                turn(0, 1)
                walk(pe, s, step, top)
                finish(seg_tiles[s])
            for tile in seg_tiles[-1]:
                top(tile)


def _unit_counts():
    tail_units, top_units = 7, 4
    h, o8, n = [], [], 0
    for s, nb in enumerate(SEGS):
        if s == 0:
            n += tail_units * nb
        if s == 1:
            n += tail_units * (BT - SEGS[0])
        h.append(n)
        if s > 0:
            n += top_units * SEGS[s - 1]
        n += 1
        o8.append([])
        for two in [range(b, min(b + 2, nb)) for b in range(0, nb, 2)]:
            n += len(two)
            o8[-1] += [n + a for a in range(len(two))]
            n += len(two)
    n += top_units * SEGS[-1]
    return h, o8, n


h_units, out8_units, total_units = _unit_counts()


def kernel(**inputs):
    import concourse.bacc as _bacc
    from concourse.bass_utils import run_bass_kernel_spmd as _run

    a = {k: np.asarray(v) for k, v in inputs.items()}
    i, j, ok = pair_indices()
    lo, hi = np.minimum(i, j), np.maximum(i, j)
    row = lo * EMB - lo * (lo + 1) // 2 + (hi - lo - 1)
    w7 = a["L0_rec_w7"][np.where(ok, row, 0)]
    w7[~ok] = 0
    w7 = w7.reshape(KT // 2, 2, P, EMB).transpose(0, 2, 1, 3).reshape(KT // 2, P, 2 * EMB)
    v = a["L0_rec_v"]

    def rows(index):
        r = v[index]
        r[~ok] = 0
        return r.transpose(1, 0, 2).reshape(P, KT * RANK)

    first = np.cumsum([0] + VOCAB[:-1])
    offs = first.reshape(XT, 2).T.repeat(HALF, axis=0)
    ids = a["ids"].reshape(2 * BT, HALF, XT, 2).transpose(3, 1, 0, 2).reshape(P, 2 * BT * XT)
    att = np.zeros((ATT, 2, P + XW), np.float32)
    for n, (wa, ba, wb) in enumerate((("w1", "b1", "w2"), ("w3", "b3", "w4"))):
        att[:, n, 0:P] = a["L0_rec_" + wb].reshape(ATT, 1)
        att[:, n, P:P + EMB] = a["L0_rec_" + wa].T
        att[:, n, P + EMB] = a["L0_rec_" + ba]
    arrays = {
        "table": np.concatenate([a[f"tbl_{n}"] for n in range(FEATS)], axis=0),
        "ids": ids, "offs": offs.astype(np.int32),
        "le": a["r_label_embedding"].reshape(BATCH, KEYS * EMB),
        "w7": w7, "vi": rows(i), "vj": rows(j), "att": att,
        "w5": a["L0_rec_w5"].reshape(6, CH, EMB).transpose(1, 0, 2),
        "w6": a["L0_rec_w6"].reshape(3, CH, EMB).transpose(1, 0, 2),
        "w8": a["L0_rec_w8"].reshape(6, CH, EMB).transpose(1, 0, 2),
        "bias": np.stack([a["L0_rec_b5"], a["L0_rec_b6"], a["L0_rec_b7"], a["L0_rec_b8"]])[None],
        "wt1": a["W_top1"].reshape(2, 108, HID1).transpose(1, 0, 2),
        "bt1": a["b_top1"].reshape(HID1 // P, P).T,
        "wt2": a["W_top2"].reshape(HID1 // P, P, HID2).transpose(1, 0, 2),
        "bt2": a["b_top2"].reshape(HID2 // P, P).T,
        "wt3": a["W_top3"].reshape(HID2 // P, P).T,
        "dense": a["dense_ctx"],
        "ident": np.eye(P, dtype=np.float32),
        "sel": np.tile(np.eye(HALF, dtype=np.float32), (2, 1)),
    }
    nc = _bacc.Bacc("TRN2", target_bir_lowering=False, num_devices=1)
    named, args = {}, []
    for name, arr in arrays.items():
        arr = np.ascontiguousarray(arr)
        named[f"in_{name}"] = arr
        args.append(nc.dram_tensor(f"in_{name}", arr.shape, mybir.dt.from_np(arr.dtype), kind="ExternalInput").ap())
    args.append(nc.dram_tensor("out_y", (1, BATCH), mybir.dt.float32, kind="ExternalOutput").ap())
    build(nc, *args)
    r = _run(nc, [named], core_ids=[0])
    return r.results[0]["out_y"].reshape(BATCH, 1)
```

```python
import concourse.bass as bass
import numpy as np
from concourse import mybir

BATCH, FEATS, EMB, KEYS = 1024, 50, 300, 200
DENSE, HID1, HID2, RANK, ATT = 16, 512, 256, 4, 8
VOCAB = [1250, 1250, 1250, 1000, 1250, 1250, 1000, 12500, 1000, 12500, 1250, 1000, 1250, 1000, 1250,
         1250, 1250, 1000, 12500, 12500, 1250, 12500, 1250, 1250, 1250, 12500, 1250, 1000, 1250, 1250,
         1000, 1250, 1000, 1000, 1000, 1000, 1250, 1250, 1250, 1000] + [1000] * 10
ROWS = sum(VOCAB)
PAD = float(np.float32(-2 ** 32 + 1))

P = 128
BT = BATCH // P
CH = EMB // 3
HALF = P // 2
XT = FEATS // 2
XB = 5
NXB = XT // XB
XW = EMB + 1

NEAR = P
FAR_D, FAR_I = EMB // 2 - 1 - NEAR, 6
FAR_T = EMB // FAR_I
OPP = EMB // 4
KT = EMB + FAR_T + 2
KI = 16
ITS = KT // KI
PR = KI // 2
WS = 4
HS = 4
MAIN_ITS = EMB // KI
H2W = EMB + EMB // 2

SEGS = [1, 4, 3]
NBM = max(SEGS)
FIRST = SEGS[0]
ATT_ITS = 2 * (BT - FIRST)
ZK = 5
ZT = KEYS // ZK
ZN = [{1: 10, 2: 20, 3: 40, 4: 40}[n] // ZK for n in SEGS]
ZN[-1] = 40 // ZK
ZSLOTS = max(ZN)
ROWS_FIRST = 22
H_UNITS = 3
TAIL = 7
TOP = 4

SPLIT = [(), tuple(range(PR)), (3, 7)]

SPLIT_NB = max([1] + [n for n, pairs in zip(SEGS, SPLIT) if pairs])
WHOLE_NB = max([1] + [n for n, pairs in zip(SEGS, SPLIT) if len(pairs) < PR])

ACC, POOLED, TBANK, MISC = 0, 3, 4, 6


def pair_indices():
    i = np.zeros((KT, P), np.int64)
    j = np.zeros((KT, P), np.int64)
    ok = np.zeros((KT, P), bool)
    for t in range(EMB):
        i[t], j[t], ok[t] = t, (t + 1 + np.arange(P)) % EMB, True
    for m in range(FAR_T):
        for a in range(FAR_I):
            s = slice(FAR_D * a, FAR_D * (a + 1))
            i[EMB + m, s] = FAR_I * m + a
            j[EMB + m, s] = (FAR_I * m + a + NEAR + 1 + np.arange(FAR_D)) % EMB
            ok[EMB + m, s] = True
    for q in range(2):
        i[EMB + FAR_T + q, :OPP] = OPP * q + np.arange(OPP)
        j[EMB + FAR_T + q, :OPP] = OPP * q + np.arange(OPP) + EMB // 2
        ok[EMB + FAR_T + q, :OPP] = True
    return i, j, ok


def build(nc, t_table, t_ids, t_offs, t_le, t_w7, t_vi, t_vj, t_att, t_w5, t_w6, t_w8, t_bias,
          t_wt1, t_bt1, t_wt2, t_bt2, t_wt3, t_dense, t_ident, t_sel, out):
    f32, f32r, i32 = mybir.dt.float32, mybir.dt.float32r, mybir.dt.int32
    ALU, ACT, AX = mybir.AluOpType, mybir.ActivationFunctionType, mybir.AxisListType

    from contextlib import ExitStack
    ctx = ExitStack()
    with ctx:
        def sb(name, shape, dt=f32):
            return ctx.enter_context(nc.sbuf_tensor(name, shape, dt))

        def sem(name):
            return ctx.enter_context(nc.semaphore(name))

        ids = sb("ids", [P, BT * 2 * XT], i32)
        offs = sb("offs", [P, XT], i32)
        idx = sb("idx", [P, 2, XT], i32)
        big = sb("big", [P, 2 * XT * XW])
        x = big[:, :].rearrange("p (s t w) -> p s t w", s=2, t=XT)
        le = big[:, 0:ZSLOTS * ZK * EMB].rearrange("p (s k u) -> p s k u", s=ZSLOTS, k=ZK)
        zc = big[:, ZSLOTS * ZK * EMB:ZSLOTS * ZK * EMB + BT * (KEYS + DENSE)].rearrange("p (t k) -> p t k", t=BT)
        pm = sb("pm", [P, XT * 2 * HALF])
        vi = pm[:, 0:KT * RANK]
        vj = pm[:, KT * RANK:2 * KT * RANK]
        gate = sb("gate", [P, KT])
        ident = sb("ident", [P, P])
        sel = sb("sel", [P, HALF])
        ones = sb("ones", [1, P])
        wv = sb("wv", [P, 2, XW])
        score = sb("score", [P, 2, XT])
        absum = sb("absum", [P, XT])
        iszero = sb("iszero", [P, XT], i32)
        padrow = sb("padrow", [P, XT])
        es = sb("es", [P, 2, XT])
        ew = sb("ew", [P, 2, XT])
        mx = sb("mx", [P, 2])
        mxo = sb("mxo", [P, 2])
        negmax = sb("negmax", [P, 2])
        rsum = sb("rsum", [P, 2])
        junkv = sb("junkv", [P, 4, EMB])
        junka = sb("junka", [P, EMB])
        f7 = sb("f7", [P, 4, EMB])
        q = f7[:, 0:2, :]
        qT = sb("qT", [CH, 3, 2, P])
        h2 = sb("h2", [P, BT, H2W])
        h, f6 = f7[:, 2, :], f7[:, 3, :]
        hT = qT[:, :, 0, :]
        featT = qT[:, :, 1, :]
        out8 = sb("out8", [P, BT, EMB])
        w5 = sb("w5", [CH, 6, EMB])
        w6 = sb("w6", [CH, 3, EMB])
        w8 = sb("w8", [CH, 6, EMB])
        bias = sb("bias", [1, 4, EMB])
        cross = sb("cross", [P, 4, NBM, P])
        w2rep = cross[0:ATT, 0:2, 0, :]
        w1row = cross[0:ATT, 2:4, :, :].rearrange("p a t b -> p a (t b)")[:, :, 0:XW]
        crossT = sb("crossT", [P, 4, WHOLE_NB, P])
        crossH = sb("crossH", [P, 4, SPLIT_NB, P], f32r)
        crossL = sb("crossL", [P, 4, SPLIT_NB, P], f32r)
        w7 = sb("w7", [P, WS, 2, EMB])
        w7H = sb("w7H", [P, HS, 2, EMB], f32r)
        w7L = sb("w7L", [P, HS, 2, EMB], f32r)
        wt1 = sb("wt1", [108, 2, HID1])
        bt1 = sb("bt1", [P, HID1 // P])
        wt2 = sb("wt2", [P, HID1 // P, HID2])
        bt2 = sb("bt2", [P, HID2 // P])
        wt3 = sb("wt3", [P, HID2 // P])
        y1 = pm[:, 0:HID1].rearrange("p (c b) -> p c b", b=P)
        y2 = pm[:, HID1:HID1 + HID2].rearrange("p (c b) -> p c b", b=P)
        zT = pm[0:108, HID1 + HID2:HID1 + HID2 + 2 * P].rearrange("p (c b) -> p c b", b=P)
        yrow = pm[0:1, 2 * BATCH:3 * BATCH]
        ps = ctx.enter_context(nc.psum_tensor("ps", [P, 8, 512], f32))

        att_in = sem("att_in")
        v_in = sem("v_in")
        const_in = sem("const_in")
        x_in = [[sem(f"x_in{s}_{b}") for b in range(NXB)] for s in range(2)]
        w7_in = [sem(f"w7_in{g}") for g in range(WS)]
        le_in = [sem(f"le_in{g}") for g in range(ZSLOTS)]
        dense_in = sem("dense_in")
        y_out = sem("y_out")
        idx_ready = sem("idx_ready")
        init_done = sem("init_done")
        wv_mm = sem("wv_mm")
        wv_ready = sem("wv_ready")
        g_step = sem("g_step")
        score_step = sem("score_step")
        abs_done = sem("abs_done")
        es_done = sem("es_done")
        att_step = sem("att_step")
        ew_done = sem("ew_done")
        pm_done = sem("pm_done")
        pooled = sem("pooled")
        rsum_done = sem("rsum_done")
        q_done = sem("q_done")
        prod = sem("prod")
        high_w7 = sem("high_w7")
        low_w7 = sem("low_w7")
        low = sem("low")
        trans = sem("trans")
        scaled = sem("scaled")
        summed = sem("summed")
        zdone = sem("zdone")
        unit_mm = sem("unit_mm")
        unit_ev = sem("unit_ev")
        sums_out = sem("sums_out")
        out8_done = sem("out8_done")

        ATT_STEPS = 6
        seg_start = [sum(SEGS[:s]) for s in range(len(SEGS))]
        seg_tiles = [list(range(a, a + n)) for a, n in zip(seg_start, SEGS)]

        block = ctx.enter_context(nc.Block())

        def finish_unit(s):
            return TAIL * BT + (2 + TOP) * seg_start[s]

        def top_unit(tile):
            s = [tile in tiles for tiles in seg_tiles].index(True)
            return finish_unit(s) + 2 * SEGS[s] + TOP * (tile - seg_start[s])

        TOTAL_UNITS = (TAIL + 2 + TOP) * BT
        TOP_K = (5, 8, 11, 14)
        TAIL_K = {"h": (1, 3, 5), "rest": (None, None, None, 1, 3, 6, 8), "all": range(0, 2 * TAIL, 2)}

        def tail_stage(part, k):
            return TAIL_K[part].index(k) if k in TAIL_K[part] else None

        def finish_stage(s, k):
            return k // 2 if k % 2 == 0 and k // 2 < 2 * SEGS[s] else None

        def run(eng, start, end, step):
            if end - start >= 4:
                with eng.Fori(0, (end - start) // 2) as r:
                    step(r * 2 + start)
                    step(r * 2 + (start + 1))
                start = end - (end - start) % 2
            for it in range(start, end):
                step(it)

        def walk(eng, s, step):
            if s == 0:
                step(0, att=(0, FIRST, "first"))
                step(1, att=(1, FIRST, "steady"))
                with eng.Fori(0, ATT_ITS // 2 - 1) as r:
                    step(r * 2 + 2, att=(0, r + (FIRST + 1), "steady"), tail=(r + (FIRST - 1), "rest"))
                    step(r * 2 + 3, att=(1, r + (FIRST + 1), "steady"), tail=(r + FIRST, "h"))
                step(ATT_ITS, att=(0, BT, "drain"), tail=(BT - 2, "rest"))
                step(ATT_ITS + 1, tail=(BT - 1, "all"))
                run(eng, ATT_ITS + 2, max(ATT_ITS + 2, MAIN_ITS), step)
                for it in range(max(ATT_ITS + 2, MAIN_ITS), ITS):
                    step(it)
                return
            step(0, fin=s - 1)
            tiles, per = seg_tiles[s - 1], ZT // ZN[s - 1]
            it = 1
            while it < ITS:
                a, b = divmod(it - 1, per)
                end = it + 1
                top = tiles[a - 1] if b == 0 and 0 < a <= len(tiles) else None
                if top is None:
                    last = per * (a + 1) + 1 if a < len(tiles) else ITS
                    end = min(last, max(end, MAIN_ITS)) if it < MAIN_ITS else end
                if end - it > 1:
                    run(eng, it, end, lambda i: step(i, z=(tiles[a], i - 1) if a < len(tiles) else None))
                else:
                    step(it, z=(tiles[a], it - 1) if a < len(tiles) else None, top=top)
                it = end

        def loads_before(s):
            return ZT * seg_start[s]

        def le_count(s, zi, g):
            before = sum(ZT * SEGS[r] // ZN[r] for r in range(s) if ZN[r] > g)
            return (zi + (before + 1)) * 16

        def fast(s, k):
            return k // 2 in SPLIT[s]

        def loaded(it, pr, s):
            return (it * (PR // WS) + (s * ITS * (PR // WS) + pr // WS + 1)) * 16

        def low_count(s, it, k):
            before = sum(len(SPLIT[r]) * 2 * ITS for r in range(s))
            if k == -1 and isinstance(it, int) and it == 0:
                return before
            return it * (len(SPLIT[s]) * 2) + (before + sum(fast(s, n) for n in range(k + 1))
                                               - sum(fast(s, KI + n) for n in range(k + 1, 0)))

        def split_count(s, it, pr):
            before = sum(len(SPLIT[r]) * ITS for r in range(s))
            return it * len(SPLIT[s]) + (before + sum(n <= pr for n in SPLIT[s])
                                         - sum(n > pr + PR for n in SPLIT[s] if pr < 0))

        def in_split(s, it, pr):
            return pr % PR in SPLIT[s] and not (pr >= PR and isinstance(it, int) and it == ITS - 1)

        @block.sync
        def _(sp):
            for dst, src in ((ids[:, :], t_ids), (offs[:, :], t_offs), (w2rep, t_att[:, :, 0:P]),
                             (w1row, t_att[:, :, P:P + XW]), (sel[:, :], t_sel),
                             (ident[:, :], t_ident), (bias[:, :, :], t_bias)):
                sp.dma_start(dst, src).then_inc(att_in, 16)
            sp.wait_ge(x_in[0][0], 16 * XB)
            sp.dma_start(vi, t_vi).then_inc(v_in, 16)
            sp.dma_start(vj, t_vj).then_inc(v_in, 16)
            sp.wait_ge(x_in[0][NXB - 1], 16 * XB)
            for dst, src in ((w5[:, :, :], t_w5), (w6[:, :, :], t_w6), (w8[:, :, :], t_w8),
                             (wt1[:, :, :], t_wt1), (bt1[:, :], t_bt1), (wt2[:, :, :], t_wt2),
                             (bt2[:, :], t_bt2), (wt3[:, :], t_wt3)):
                sp.dma_start(dst, src).then_inc(const_in, 16)

            for s, nb in enumerate(SEGS):
                def step(it, s=s, **beside):
                    for pr in range(PR):
                        last = pr - WS
                        if s > 0 or not isinstance(it, int) or it > 0 or last >= 0:
                            fresh = isinstance(it, int) and it == 0 and last < 0
                            if last % PR in SPLIT[s] and not fresh:
                                sp.wait_ge(low_w7, split_count(s, it, last))
                            else:
                                sp.wait_ge(summed, (it + s * ITS) * KI + 2 * (last + 1))
                            nc.sync.nop(nofuse=True)
                        sp.dma_start(w7[:, pr % WS, :, :].rearrange("p k u -> p (k u)"),
                                     t_w7[bass.ds(it * PR + pr, 1), :, :].rearrange("a p n -> (a p) n")
                                     ).then_inc(w7_in[pr % WS], 16)
                walk(sp, s, step)
            sp.wait_ge(unit_ev, TOTAL_UNITS)
            sp.dma_start(out, yrow).then_inc(y_out, 16)
            sp.wait_ge(y_out, 16)

        @block.gpsimd
        def _(pool):
            nc.gpsimd.memset(ones[:, :], 1.0).then_inc(init_done, 1)
            nc.gpsimd.memset(padrow[:, :], PAD).then_inc(init_done, 1)
            nc.gpsimd.memset(x[:, :, :, EMB:XW], 1.0).then_inc(init_done, 1)
            pool.wait_ge(att_in, 7 * 16)

            def gather(slot, m, first):
                n = m * 2 + slot
                if not first:
                    pool.wait_ge(pooled, n * NXB - (2 * NXB - 1))
                nc.gpsimd.tensor_tensor(idx[:, slot, :], ids[:, bass.ds(n * XT, XT)], offs[:, :],
                                        ALU.add).then_inc(idx_ready, 1)
                pool.wait_ge(idx_ready, n + 1)
                for b in range(NXB):
                    if not first and b:
                        pool.wait_ge(pooled, n * NXB - (2 * NXB - b - 1))
                    nc.gpsimd.nop(nofuse=True)
                    for t in range(XB * b, XB * (b + 1)):
                        nc.gpsimd.indirect_dma_start(
                            out=x[:, slot, t, 0:EMB], out_offset=None, in_=t_table,
                            in_offset=bass.IndirectOffsetOnAxis(ap=idx[:, slot, t:t + 1], axis=0),
                        ).then_inc(x_in[slot][b], 16)

            gather(0, 0, True)
            gather(1, 0, True)
            with pool.Fori(1, BT) as m:
                gather(0, m, False)
                gather(1, m, False)

            def load_le(s, zi, tile):
                for g in range(ZN[s]):
                    if not isinstance(zi, int) or zi > 0:
                        pool.wait_ge(zdone, zi * ZN[s] + (loads_before(s) + g + 1 - ZN[s]))
                    key = (zi * ZN[s] + (g - ZT * (tile - seg_start[s]))) * (ZK * EMB)
                    rows = t_le[tile * P:(tile + 1) * P, bass.ds(key, ZK * EMB)]
                    pool.dma_start(le[:, g, :, :].rearrange("p k u -> p (k u)"), rows).then_inc(le_in[g], 16)

            pool.wait_ge(pooled, 2 * BT * NXB)
            pool.dma_start(zc[:, :, KEYS:], t_dense.rearrange("(t p) c -> p t c", p=P)).then_inc(dense_in, 16)
            for s in range(len(SEGS)):
                if s > 0:
                    pool.wait_ge(zdone, loads_before(s))
                load_le(s, 0, seg_start[s])
                for a, tile in enumerate(seg_tiles[s]):
                    with pool.Fori(a * (ZT // ZN[s]) + (a == 0), (a + 1) * (ZT // ZN[s])) as zi:
                        load_le(s, zi, tile)

        @block.vector
        def _(dve):
            def scores(slot, m, ts):
                for t in ts:
                    if t == 0 and (not isinstance(m, int) or 2 * m + slot > 0):
                        dve.wait_ge(es_done, m * 2 + slot)
                    if t % XB == 0:
                        dve.wait_ge(x_in[slot][t // XB], (m + 1) * (16 * XB))
                    if not isinstance(m, int) or 2 * m + slot > 0 or t > 1:
                        dve.wait_ge(score_step, (m * 2 + slot) * XT + (t - 1))
                    for head in range(2):
                        last = nc.vector.scalar_tensor_tensor(
                            junkv[:, 2 * ((t + slot) % 2) + head, :], x[:, slot, t, 0:EMB], 1.0,
                            wv[:, head, 0:EMB], ALU.mult, ALU.mult, accum_out=score[:, head, t:t + 1])
                    last.then_inc(score_step, 1)

            def maxima(slot, m):
                n = m * 2 + slot
                dve.wait_ge(abs_done, (n + 1) * XT)
                nc.vector.tensor_scalar(iszero[:, :], absum[:, :], 0.0, None, ALU.is_equal).then_inc(att_step, 1)
                dve.wait_ge(att_step, n * ATT_STEPS + 1)
                dve.wait_ge(es_done, n + 1)
                nc.vector.nop(nofuse=True)
                for head in range(2):
                    last = nc.vector.copy_predicated(es[:, head, :], iszero[:, :], padrow[:, :])
                last.then_inc(att_step, 1)
                dve.wait_ge(att_step, n * ATT_STEPS + 2)
                nc.vector.reduce_max(mx[:, :], es[:, :, :], AX.X).then_inc(att_step, 1)
                dve.wait_ge(att_step, n * ATT_STEPS + 3)
                nc.vector.tensor_copy(mxo[0:HALF, :], mx[HALF:P, :])
                nc.vector.tensor_copy(mxo[HALF:P, :], mx[0:HALF, :]).then_inc(att_step, 1)
                dve.wait_ge(att_step, n * ATT_STEPS + 4)
                nc.vector.tensor_tensor(mxo[:, :], mx[:, :], mxo[:, :], ALU.max).then_inc(att_step, 1)
                dve.wait_ge(att_step, n * ATT_STEPS + 5)
                nc.vector.tensor_scalar(negmax[:, :], mxo[:, :], -1.0, None, ALU.mult).then_inc(att_step, 1)

            def reciprocal(slot, m):
                dve.wait_ge(pooled, m * (2 * NXB) + (slot + 1) * NXB)
                nc.vector.reciprocal(rsum[:, slot:slot + 1], ps[:, POOLED, EMB:XW]).then_inc(rsum_done, 1)

            def spread(slot, m, part):
                n = m * 2 + slot
                lo, hi = ((0, 7), (7, 13), (13, 19), (19, XT))[part]
                if part == 0:
                    dve.wait_ge(ew_done, n + 1)
                    if not isinstance(n, int) or n > 0:
                        dve.wait_ge(pooled, n * NXB)
                    else:
                        dve.wait_ge(g_step, 2)
                pv = pm[:, :].rearrange("p (t h b) -> p t h b", t=XT, h=2)[:, lo:hi, :, :]
                e = ew[:, :, lo:hi]
                ev = bass.AP(e.tensor, e.offset, [e.ap[0], [1, hi - lo], [XT, 2], [0, HALF]])
                sv = sel[:, :]
                sv = bass.AP(sv.tensor, sv.offset, [sv.ap[0], [0, hi - lo], [0, 2], [1, HALF]])
                nc.vector.tensor_tensor(pv, ev, sv, ALU.mult).then_inc(pm_done, 1)

            dve.wait_ge(wv_ready, 1)
            dve.wait_ge(init_done, 3)

            def attend(slot, m, first):
                scores(slot, m, range(ROWS_FIRST))
                if not first:
                    reciprocal(1 - slot, m if slot else m - 1)
                if first:
                    dve.wait_ge(v_in, 32)
                    nc.vector.tensor_tensor(vi, vi, vj, ALU.mult).then_inc(g_step, 1)
                    dve.wait_ge(g_step, 1)
                    nc.vector.reduce_sum(gate[:, :], vi.rearrange("p (t c) -> p t c", c=RANK), AX.X
                                         ).then_inc(g_step, 1)
                scores(slot, m, range(ROWS_FIRST, XT))
                maxima(slot, m)
                for part in range(4):
                    spread(slot, m, part)
            attend(0, 0, True)
            attend(1, 0, False)
            for m in range(1, FIRST):
                attend(0, m, False)
                attend(1, m, False)
            reciprocal(1, FIRST - 1)

            def key_scores(s, tile, zi, keys):
                for n in keys:
                    g, k = divmod(n, ZK)
                    if n == 0:
                        dve.wait_ge(out8_done, tile + 1)
                    if k == 0:
                        dve.wait_ge(le_in[g], le_count(s, zi, g))
                    key = (zi * ZN[s] + (g - ZT * (tile - seg_start[s]))) * ZK + k
                    last = nc.vector.scalar_tensor_tensor(
                        le[:, g, k, :], le[:, g, k, :], 1.0, out8[:, tile, :], ALU.mult, ALU.mult,
                        accum_out=zc[:, tile, bass.ds(key, 1)])
                    if k == ZK - 1:
                        last.then_inc(zdone, 1)

            def finish_out8(s, b):
                dve.wait_ge(unit_ev, finish_unit(s) + 2 * b + 2)
                tile = seg_start[s] + b
                nc.vector.tensor_tensor(out8[:, tile, :], f7[:, b, :], out8[:, tile, :], ALU.add).then_inc(out8_done, 1)

            for s, nb in enumerate(SEGS):
                t0 = seg_start[s]
                dve.wait_ge(unit_ev, TAIL * seg_tiles[s][-1] + H_UNITS)

                def products(it, pr, s=s, nb=nb, t0=t0):
                    sl = (2 * pr) % 4
                    k = 2 * pr
                    if s > 0 or not isinstance(it, int) or it > 0 or k >= 4:
                        dve.wait_ge(trans, (it + s * ITS) * KI + (k - 2))
                    if not isinstance(it, int) or it * KI + k < EMB:
                        hi = h2[:, t0, bass.ds(it * KI + k, 1)]
                        hj = h2[:, t0, bass.ds(it * KI + k + 1, 1)]
                        dst = cross[:, sl, 0, 0:1]
                        nc.vector.tensor_tensor(
                            bass.AP(dst.tensor, dst.offset, [dst.ap[0], [NBM * P, 2], [P, nb], [1, P]]),
                            bass.AP(hi.tensor, hi.offset, [hi.ap[0], [1, 2], [H2W, nb], [0, P]]),
                            bass.AP(hj.tensor, hj.offset, [hj.ap[0], [1, 2], [H2W, nb], [1, P]]),
                            ALU.mult).then_inc(prod, 1)
                        return
                    for a in range(2):
                        kt = it * KI + k + a
                        dst = cross[:, sl + a, 0, 0:1]
                        if kt < EMB + FAR_T:
                            i0 = FAR_I * (kt - EMB)
                            dims = ([P, nb], [FAR_D, FAR_I], [1, FAR_D])
                            idim = ([H2W, nb], [1, FAR_I], [0, FAR_D])
                            jdim = ([H2W, nb], [1, FAR_I], [1, FAR_D])
                            j0 = i0 + NEAR + 1
                        else:
                            i0 = OPP * (kt - EMB - FAR_T)
                            dims = ([P, nb], [1, OPP])
                            idim = jdim = ([H2W, nb], [1, OPP])
                            j0 = i0 + EMB // 2
                        hi = h2[:, t0, i0:i0 + 1]
                        hj = h2[:, t0, j0:j0 + 1]
                        last = nc.vector.tensor_tensor(
                            bass.AP(dst.tensor, dst.offset, [dst.ap[0], *dims]),
                            bass.AP(hi.tensor, hi.offset, [hi.ap[0], *idim]),
                            bass.AP(hj.tensor, hj.offset, [hj.ap[0], *jdim]), ALU.mult)
                    last.then_inc(prod, 1)

                def low_part(it, k, s=s, nb=nb):
                    kt = it * KI + k
                    dve.wait_ge(scaled, kt + (s * KT + 1))
                    nc.vector.scalar_tensor_tensor(
                        crossL[:, k % 4, 0:nb, :].rearrange("p t b -> p (t b)"),
                        ps[:, TBANK + k % 2, 0:nb * P], gate[:, bass.ds(kt, 1)],
                        crossH[:, k % 4, 0:nb, :].rearrange("p t b -> p (t b)").bitcast(f32),
                        ALU.mult, ALU.subtract).then_inc(low, 1)

                def low_weights(it, pr, s=s):
                    dve.wait_ge(high_w7, split_count(s, it, pr))
                    nc.vector.tensor_tensor(w7L[:, pr % HS, :, :], w7[:, pr % WS, :, :],
                                            w7H[:, pr % HS, :, :].bitcast(f32), ALU.subtract).then_inc(low_w7, 1)

                def step(it, att=None, tail=None, z=None, fin=None, top=None, s=s):
                    for k in range(KI):
                        if fast(s, k):
                            low_part(it, k)
                        if k % 2 and in_split(s, it, (k + 3) // 2):
                            low_weights(it + (k + 3) // KI, (k + 3) // 2 % PR)
                        if fin is not None:
                            for b in range(SEGS[fin]):
                                if k == min(4 * b + 6, KI - 1):
                                    finish_out8(fin, b)
                        if z:
                            n = ZN[s - 1] * ZK
                            key_scores(s - 1, *z, range(n * k // KI, n * (k + 1) // KI))
                        if k % 2 == 0:
                            ahead, pr = (k + 4) // KI, (k + 4) % KI // 2
                            if not (isinstance(it, int) and it + ahead == ITS):
                                products(it + ahead, pr)
                        if att:
                            slot, m, kind = att
                            if kind != "drain":
                                scores(slot, m, range(2 * k, min(2 * k + 2, XT)))
                                if k == 13:
                                    maxima(slot, m)
                            if k == 14 and kind != "first":
                                reciprocal(1 - slot, m if slot else m - 1)
                            if k >= 14 and kind != "drain":
                                for part in (2 * k - 28, 2 * k - 27):
                                    spread(slot, m, part)

                products(0, 0)
                products(0, 1)
                for pr in (0, 1):
                    if pr in SPLIT[s]:
                        low_weights(0, pr)
                walk(dve, s, step)
            last = len(SEGS) - 1
            for a, tile in enumerate(seg_tiles[last]):
                finish_out8(last, a)
                with dve.Fori(a * (ZT // ZN[last]), (a + 1) * (ZT // ZN[last])) as zi:
                    key_scores(last, tile, zi, range(ZN[last] * ZK))

        @block.scalar
        def _(act):
            def absolutes(slot, m, ts):
                for t in ts:
                    if t % XB == 0:
                        act.wait_ge(x_in[slot][t // XB], (m + 1) * (16 * XB))
                    if t == 0 and (not isinstance(m, int) or 2 * m + slot > 0):
                        act.wait_ge(att_step, (m * 2 + slot) * ATT_STEPS - (ATT_STEPS - 1))
                    if not isinstance(m, int) or 2 * m + slot > 0 or t > 0:
                        act.wait_ge(abs_done, (m * 2 + slot) * XT + t)
                    nc.scalar.activation(junka[:, :], x[:, slot, t, 0:EMB], ACT.Abs,
                                         accum_out=absum[:, t:t + 1]).then_inc(abs_done, 1)

            def exp_scores(slot, m):
                n = m * 2 + slot
                act.wait_ge(score_step, (n + 1) * XT)
                if not isinstance(n, int) or n > 0:
                    act.wait_ge(ew_done, n)
                for head in range(2):
                    last = nc.scalar.activation(es[:, head, :], score[:, head, :], ACT.Exp,
                                                bias=wv[:, head, EMB:XW])
                last.then_inc(es_done, 1)

            def exp_weights(slot, m):
                n = m * 2 + slot
                act.wait_ge(att_step, (n + 1) * ATT_STEPS)
                if not isinstance(n, int) or n > 0:
                    act.wait_ge(pm_done, n * 4)
                for head in range(2):
                    last = nc.scalar.activation(ew[:, head, :], es[:, head, :], ACT.Exp,
                                                bias=negmax[:, head:head + 1])
                last.then_inc(ew_done, 1)

            def normalise(slot, m):
                n = m * 2 + slot
                act.wait_ge(rsum_done, n + 1)
                nc.scalar.activation(q[:, slot, :], ps[:, POOLED, 0:EMB],
                                     ACT.Copy, scale=rsum[:, slot:slot + 1]).then_inc(q_done, 1)

            def evacuate(u, outs):
                act.wait_ge(unit_mm, u + 1)
                for dst, src in outs:
                    last = nc.scalar.activation(dst, src, ACT.Copy)
                last.then_inc(unit_ev, 1)

            def tail_unit(tile, j):
                bank = MISC + j % 2
                blocks = ps[0:CH, bank, 0:3 * P].rearrange("p (c b) -> p c b", c=3)
                rows = ps[:, bank, 0:EMB]
                if j < 2:
                    outs = [(qT[:, :, :, j * HALF:(j + 1) * HALF],
                             ps[0:CH, bank, 0:3 * P].rearrange("p (c h b) -> p c h b", c=3, h=2))]
                elif j == 2:
                    own = h2[:, bass.ds(tile, 1), :].rearrange("p a e -> p (a e)")
                    outs = [(h, rows), (own[:, 0:EMB], rows), (own[:, EMB:H2W], ps[:, bank, 0:H2W - EMB])]
                elif j == 4:
                    outs = [(f6, rows)]
                elif j == 6:
                    outs = [(out8[:, bass.ds(tile, 1), :].rearrange("p a e -> p (a e)"), rows)]
                else:
                    outs = [(hT if j == 3 else featT, blocks)]
                evacuate(tile * TAIL + j, outs)

            def sums_of(s):
                act.wait_ge(summed, (s + 1) * KT)
                if s > 0:
                    act.wait_ge(out8_done, seg_start[s])
                for b in range(SEGS[s]):
                    last = nc.scalar.activation(f7[:, b, :], ps[:, ACC + b, 0:EMB], ACT.Copy)
                last.then_inc(sums_out, 1)

            def fin_unit(s, j):
                bank = MISC + j % 2
                if j % 2 == 0:
                    evacuate(finish_unit(s) + j, [(featT, ps[0:CH, bank, 0:3 * P].rearrange("p (c b) -> p c b", c=3))])
                else:
                    evacuate(finish_unit(s) + j, [(f7[:, j // 2, :], ps[:, bank, 0:EMB])])

            def top_stage(tile, j):
                u, bank = top_unit(tile) + j, MISC + j % 2
                if j == 0:
                    evacuate(u, [(zT, ps[0:108, bank, 0:2 * P].rearrange("p (c b) -> p c b", c=2))])
                elif j == TOP - 1:
                    evacuate(u, [(yrow[0:1, tile * P:(tile + 1) * P], ps[0:1, bank, 0:P])])
                else:
                    dst, b_, n = ((y1, bt1, HID1 // P), (y2, bt2, HID2 // P))[j - 1]
                    act.wait_ge(unit_mm, u + 1)
                    for c in range(n):
                        last = nc.scalar.activation(dst[:, c, :], ps[:, bank, c * P:(c + 1) * P], ACT.Relu,
                                                    bias=b_[:, c:c + 1])
                    last.then_inc(unit_ev, 1)

            act.wait_ge(wv_mm, 1)
            nc.scalar.activation(wv[:, :, :], ps[:, 0:2, 0:XW], ACT.Copy).then_inc(wv_ready, 1)
            act.wait_ge(wv_ready, 1)

            def attend(slot, m, first, tail=None):
                absolutes(slot, m, range(ROWS_FIRST))
                if tail is None:
                    if not first:
                        normalise(1 - slot, m if slot else m - 1)
                    absolutes(slot, m, range(ROWS_FIRST, XT))
                    exp_scores(slot, m)
                    exp_weights(slot, m)
                    return
                absolutes(slot, m, range(ROWS_FIRST, XT))
                for j in (0, 1):
                    tail_unit(tail, j)
                normalise(1 - slot, m if slot else m - 1)
                for j in (2, 3):
                    tail_unit(tail, j)
                exp_scores(slot, m)
                tail_unit(tail, 4)
                exp_weights(slot, m)
                for j in (5, 6):
                    tail_unit(tail, j)
            attend(0, 0, True)
            attend(1, 0, False)
            for m in range(1, FIRST):
                attend(0, m, False)
                attend(1, m, False, m - 1)
            normalise(1, FIRST - 1)
            for j in range(H_UNITS):
                tail_unit(FIRST - 1, j)
            act.wait_ge(g_step, 2)

            for s, nb in enumerate(SEGS):
                def scale(it, k, s=s, nb=nb):
                    kt = it * KI + k
                    act.wait_ge(trans, kt + (s * KT + 1))
                    if s > 0 or not isinstance(it, int) or it > 0 or k >= 4:
                        act.wait_ge(summed, kt + (s * KT - 3))
                    dst = crossH if fast(s, k) else crossT
                    nc.scalar.activation(dst[:, k % 4, 0:nb, :].rearrange("p t b -> p (t b)"),
                                         ps[:, TBANK + k % 2, 0:nb * P], ACT.Copy,
                                         scale=gate[:, bass.ds(kt, 1)]).then_inc(scaled, 1)

                def high_weights(it, pr, s=s):
                    act.wait_ge(w7_in[pr % WS], loaded(it, pr, s))
                    if s > 0 or not isinstance(it, int) or it > 0 or pr >= HS:
                        act.wait_ge(summed, it * KI + (s * KT + 2 * (pr - HS + 1)))
                    nc.scalar.activation(w7H[:, pr % HS, :, :], w7[:, pr % WS, :, :], ACT.Copy).then_inc(high_w7, 1)

                def step(it, att=None, tail=None, z=None, fin=None, top=None, s=s):
                    for k in range(KI):
                        scale(it, k)
                        if k % 2 == 0 and in_split(s, it, (k + 4) // 2):
                            high_weights(it + (k + 4) // KI, (k + 4) // 2 % PR)
                        if tail is not None and tail_stage(tail[1], k - 1) is not None:
                            tail_unit(tail[0], tail_stage(tail[1], k - 1))
                        if fin is not None and finish_stage(fin, k - 1) is not None:
                            fin_unit(fin, finish_stage(fin, k - 1))
                        if top is not None and k - 1 in TOP_K:
                            top_stage(top, TOP_K.index(k - 1))
                        if att:
                            slot, m, kind = att
                            if kind != "drain":
                                absolutes(slot, m, range(2 * k, min(2 * k + 2, XT)))
                                if k == 12:
                                    exp_scores(slot, m)
                                if k == 13:
                                    exp_weights(slot, m)
                            if k == 14 and kind != "first":
                                normalise(1 - slot, m if slot else m - 1)

                if s > 0:
                    sums_of(s - 1)
                for pr in (0, 1):
                    if pr in SPLIT[s]:
                        high_weights(0, pr)
                walk(act, s, step)
            last = len(SEGS) - 1
            sums_of(last)
            for j in range(2 * SEGS[last]):
                fin_unit(last, j)
            for tile in seg_tiles[last]:
                for j in range(TOP):
                    top_stage(tile, j)

        @block.tensor
        def _(pe):
            pe.wait_ge(att_in, 7 * 16)
            for head in range(2):
                last = nc.tensor.matmul(ps[:, head, 0:XW], w2rep[:, head, :], w1row[:, head, :],
                                        start=True, stop=True)
            last.then_inc(wv_mm, 1)

            def pool_rows(slot, m, ts):
                n = m * 2 + slot
                pmv = pm[:, :].rearrange("p (t m) -> p t m", t=XT)
                for t in ts:
                    if t == 0:
                        pe.wait_ge(pm_done, n * 4 + 4)
                        if not isinstance(n, int) or n > 0:
                            pe.wait_ge(q_done, n)
                    last = nc.tensor.matmul(ps[:, POOLED, 0:XW], pmv[:, t, :], x[:, slot, t, :],
                                            start=(t == 0), stop=(t == XT - 1))
                    if t % XB == XB - 1:
                        last.then_inc(pooled, 1)

            def ready(u):
                if not isinstance(u, int) or u > 0:
                    pe.wait_ge(unit_ev, u)

            def transposes(bank, src):
                for c in range(3):
                    last = nc.tensor.transpose(ps[0:CH, bank, c * P:(c + 1) * P],
                                               src[:, c * CH:(c + 1) * CH], ident[:, :])
                last.then_inc(unit_mm, 1)

            def small_products(bank, b_, terms):
                if b_ is not None:
                    nc.tensor.matmul(ps[:, bank, 0:EMB], ones[:, :], bias[:, b_, :], start=True, stop=False)
                for a, (lhs, rhs) in enumerate(terms):
                    last = nc.tensor.matmul(ps[:, bank, 0:EMB], lhs, rhs, start=(b_ is None and a == 0),
                                            stop=(a == len(terms) - 1))
                last.then_inc(unit_mm, 1)

            def tail_unit(tile, j):
                bank = MISC + j % 2
                if j == 0:
                    pe.wait_ge(q_done, tile * 2 + 2)
                if j != 1:
                    ready(tile * TAIL + j)
                if j < 2:
                    transposes(bank, q[:, j, :])
                elif j == 2:
                    small_products(bank, 0, [(qT[:, c, head, :], w5[:, 3 * head + c, :])
                                             for head in range(2) for c in range(3)])
                elif j == 4:
                    small_products(bank, 1, [(hT[:, c, :], w6[:, c, :]) for c in range(3)])
                elif j == 6:
                    small_products(bank, 3, [(featT[:, c, :], w8[:, c, :]) for c in range(3)])
                else:
                    transposes(bank, h if j == 3 else f6)

            def fin_unit(s, j):
                ready(finish_unit(s) + j)
                if j == 0:
                    pe.wait_ge(sums_out, s + 1)
                if j % 2 == 0:
                    transposes(MISC, f7[:, j // 2, :])
                else:
                    small_products(MISC + 1, None, [(featT[:, c, :], w8[:, 3 + c, :]) for c in range(3)])

            def top_stage(tile, j):
                bank = MISC + j % 2
                ready(top_unit(tile) + j)
                if j == 0:
                    pe.wait_ge(zdone, (tile + 1) * ZT)
                    pe.wait_ge(dense_in, 16)
                    for c in range(2):
                        last = nc.tensor.transpose(ps[0:108, bank, c * P:(c + 1) * P],
                                                   zc[:, tile, c * 108:(c + 1) * 108], ident[:, :])
                elif j == TOP - 1:
                    for k in range(HID2 // P):
                        last = nc.tensor.matmul(ps[0:1, bank, 0:P], wt3[:, k:k + 1], y2[:, k, :],
                                                start=(k == 0), stop=(k == HID2 // P - 1))
                else:
                    src, w, kn, mn = ((zT, wt1, 2, HID1 // P), (y1, wt2, HID1 // P, HID2 // P))[j - 1]
                    for m in range(mn):
                        for k in range(kn):
                            last = nc.tensor.matmul(ps[:, bank, m * P:(m + 1) * P], w[:, k, m * P:(m + 1) * P],
                                                    src[:, k, :], start=(k == 0), stop=(k == kn - 1))
                last.then_inc(unit_mm, 1)

            pe.wait_ge(wv_ready, 1)
            pe.wait_ge(init_done, 3)
            pool_rows(0, 0, range(XT))
            pool_rows(1, 0, range(XT))
            pe.wait_ge(const_in, 8 * 16)
            for m in range(1, FIRST):
                pool_rows(0, m, range(XT))
                for j in range(TAIL):
                    tail_unit(m - 1, j)
                pool_rows(1, m, range(XT))
            for j in range(H_UNITS):
                tail_unit(FIRST - 1, j)

            for s, nb in enumerate(SEGS):
                def turn(it, k, s=s, nb=nb):
                    kt = it * KI + k
                    if k % 2 == 0:
                        pe.wait_ge(prod, it * PR + (s * ITS * PR + k // 2 + 1))
                    if s > 0 or not isinstance(it, int) or it > 0 or k >= 2:
                        pe.wait_ge(scaled, kt + (s * KT - 1))
                        if isinstance(it, int) and it == 0 and k < 2:
                            if low_count(s, 0, -1):
                                pe.wait_ge(low, low_count(s, 0, -1))
                        elif fast(s, (k - 2) % KI):
                            pe.wait_ge(low, low_count(s, it, k - 2))
                    for b in range(nb):
                        last = nc.tensor.transpose(ps[:, TBANK + k % 2, b * P:(b + 1) * P],
                                                   cross[:, k % 4, b, :], ident[:, :])
                    last.then_inc(trans, 1)

                def add(it, k, stop=False, s=s, nb=nb):
                    kt = it * KI + k
                    if fast(s, k):
                        pe.wait_ge(low, low_count(s, it, k))
                        if k % 2 == 0:
                            pe.wait_ge(low_w7, split_count(s, it, k // 2))
                        wh, wl = (w[:, k // 2 % HS, k % 2, :] for w in (w7H, w7L))
                        for b in range(nb):
                            hi, lo = crossH[:, k % 4, b, :], crossL[:, k % 4, b, :]
                            for lhs, rhs, end in ((hi, wh, False), (hi, wl, False), (lo, wh, True)):
                                last = nc.tensor.matmul(ps[:, ACC + b, 0:EMB], lhs, rhs, start=False,
                                                        stop=(stop and end))
                    else:
                        pe.wait_ge(scaled, kt + (s * KT + 1))
                        if k % 2 == 0:
                            pe.wait_ge(w7_in[k // 2 % WS], loaded(it, k // 2, s))
                        for b in range(nb):
                            last = nc.tensor.matmul(ps[:, ACC + b, 0:EMB], crossT[:, k % 4, b, :],
                                                    w7[:, k // 2 % WS, k % 2, :], start=False, stop=stop)
                    last.then_inc(summed, 1)

                def step(it, att=None, tail=None, z=None, fin=None, top=None, s=s):
                    for k in range(KI):
                        last_it = isinstance(it, int) and it == ITS - 1
                        if not (last_it and k >= KI - 2):
                            turn(it + (k + 2) // KI, (k + 2) % KI)
                        add(it, k, stop=(last_it and k == KI - 1))
                        if tail is not None and tail_stage(tail[1], k) is not None:
                            tail_unit(tail[0], tail_stage(tail[1], k))
                        if fin is not None and finish_stage(fin, k) is not None:
                            fin_unit(fin, finish_stage(fin, k))
                        if top is not None and k in TOP_K:
                            top_stage(top, TOP_K.index(k))
                        if att and att[2] != "first" and k >= 1:
                            slot, m, kind = att
                            pool_rows(1 - slot, m if slot else m - 1, range(2 * k - 2, min(2 * k, XT)))

                turn(0, 0)
                turn(0, 1)
                if s > 0:
                    pe.wait_ge(sums_out, s)
                for b in range(nb):
                    nc.tensor.matmul(ps[:, ACC + b, 0:EMB], ones[:, :], bias[:, 2, :], start=True, stop=False)
                walk(pe, s, step)
            last = len(SEGS) - 1
            for j in range(2 * SEGS[last]):
                fin_unit(last, j)
            for tile in seg_tiles[last]:
                for j in range(TOP):
                    top_stage(tile, j)


def kernel(**inputs):
    import concourse.bacc as _bacc
    from concourse.bass_utils import run_bass_kernel_spmd as _run

    a = {k: np.asarray(v) for k, v in inputs.items()}
    i, j, ok = pair_indices()
    lo, hi = np.minimum(i, j), np.maximum(i, j)
    row = lo * EMB - lo * (lo + 1) // 2 + (hi - lo - 1)
    w7 = a["L0_rec_w7"][np.where(ok, row, 0)]
    w7[~ok] = 0
    w7 = w7.reshape(KT // 2, 2, P, EMB).transpose(0, 2, 1, 3).reshape(KT // 2, P, 2 * EMB)
    v = a["L0_rec_v"]

    def rows(index):
        r = v[index]
        r[~ok] = 0
        return r.transpose(1, 0, 2).reshape(P, KT * RANK)

    first = np.cumsum([0] + VOCAB[:-1])
    offs = first.reshape(XT, 2).T.repeat(HALF, axis=0)
    ids = a["ids"].reshape(2 * BT, HALF, XT, 2).transpose(3, 1, 0, 2).reshape(P, 2 * BT * XT)
    att = np.zeros((ATT, 2, P + XW), np.float32)
    for n, (wa, ba, wb) in enumerate((("w1", "b1", "w2"), ("w3", "b3", "w4"))):
        att[:, n, 0:P] = a["L0_rec_" + wb].reshape(ATT, 1)
        att[:, n, P:P + EMB] = a["L0_rec_" + wa].T
        att[:, n, P + EMB] = a["L0_rec_" + ba]
    arrays = {
        "table": np.concatenate([a[f"tbl_{n}"] for n in range(FEATS)], axis=0),
        "ids": ids, "offs": offs.astype(np.int32),
        "le": a["r_label_embedding"].reshape(BATCH, KEYS * EMB),
        "w7": w7, "vi": rows(i), "vj": rows(j), "att": att,
        "w5": a["L0_rec_w5"].reshape(6, CH, EMB).transpose(1, 0, 2),
        "w6": a["L0_rec_w6"].reshape(3, CH, EMB).transpose(1, 0, 2),
        "w8": a["L0_rec_w8"].reshape(6, CH, EMB).transpose(1, 0, 2),
        "bias": np.stack([a["L0_rec_b5"], a["L0_rec_b6"], a["L0_rec_b7"], a["L0_rec_b8"]])[None],
        "wt1": a["W_top1"].reshape(2, 108, HID1).transpose(1, 0, 2),
        "bt1": a["b_top1"].reshape(HID1 // P, P).T,
        "wt2": a["W_top2"].reshape(HID1 // P, P, HID2).transpose(1, 0, 2),
        "bt2": a["b_top2"].reshape(HID2 // P, P).T,
        "wt3": a["W_top3"].reshape(HID2 // P, P).T,
        "dense": a["dense_ctx"],
        "ident": np.eye(P, dtype=np.float32),
        "sel": np.tile(np.eye(HALF, dtype=np.float32), (2, 1)),
    }
    nc = _bacc.Bacc("TRN2", target_bir_lowering=False, num_devices=1)
    named, args = {}, []
    for name, arr in arrays.items():
        arr = np.ascontiguousarray(arr)
        named[f"in_{name}"] = arr
        args.append(nc.dram_tensor(f"in_{name}", arr.shape, mybir.dt.from_np(arr.dtype), kind="ExternalInput").ap())
    args.append(nc.dram_tensor("out_y", (1, BATCH), mybir.dt.float32, kind="ExternalOutput").ap())
    build(nc, *args)
    r = _run(nc, [named], core_ids=[0])
    return r.results[0]["out_y"].reshape(BATCH, 1)
```
